# Optimizing a Trainium2 kernel written in Bass

```python
import numpy as np
import jax
import jax.numpy as jnp

def _softmax(x, axis=-1):
    return jax.nn.softmax(x, axis=axis)

def _gelu(x):
    return jax.nn.gelu(x, approximate=True)

def _silu(x):
    return jax.nn.silu(x)

def _sigmoid(x):
    return jax.nn.sigmoid(x)

def _layernorm(x, axis=-1, eps=1e-05):
    m = jnp.mean(x, axis=axis, keepdims=True)
    v = jnp.var(x, axis=axis, keepdims=True)
    return (x - m) / jnp.sqrt(v + eps)

def _scatter_add(tgt, idx, src, axis=0):
    return tgt.at[idx].add(src)

def _segment_sum(src, seg, n):
    return jax.ops.segment_sum(src, seg, n)
kernel_name = 'mk_decoder_preln_d4_seqx_r8_326c61'

def setup_inputs(seed: int=0):
    np.random.seed(seed)
    _w = jnp.asarray

    def _rec_inputs():
        import jax
        import jax.numpy as jnp
        _rk = jax.random.key(seed)
        x = 7.22e-05 + 1 * jax.random.normal(jax.random.fold_in(_rk, 1), (64, 64, 128), jnp.float32)
        _lenS = 64 - jax.random.randint(jax.random.fold_in(_rk, 7), (64,), 0, max(1, 64 // 4) + 1, jnp.int32)
        _lenS2 = 64 - jax.random.randint(jax.random.fold_in(_rk, 8), (64,), 0, max(1, 64 // 4) + 1, jnp.int32)
        _ctx_1024P = jax.random.normal(jax.random.fold_in(_rk, 11), (64, 16, 128), jnp.float32)
        _ctx_1024c = jax.random.dirichlet(jax.random.fold_in(_rk, 511), 0.3 * jnp.ones((16,), jnp.float32), (64, 64))
        _ctx_1024t = jnp.einsum('bsk,bkd->bsd', _ctx_1024c, _ctx_1024P)
        _ctx_1024t = _ctx_1024t * jax.lax.rsqrt(jnp.mean(jnp.square(_ctx_1024t)) + 1e-12) * 0.953939
        ctx_1024 = 4.13588e-05 + 0.999923 * (_ctx_1024t + 0.3 * jax.random.normal(jax.random.fold_in(_rk, 611), (64, 64, 128), jnp.float32))
        _validS = jnp.arange(64)[None, :] < _lenS[:, None]
        _validS2 = jnp.arange(64)[None, :] < _lenS2[:, None]
        _causal = jnp.tril(jnp.ones((64, 64), dtype=bool))
        mask_BxS2_ff1 = jnp.where(jnp.ones((64, 64), dtype=bool), 1.0, 0.0).astype(jnp.float32)
        return (x, ctx_1024, mask_BxS2_ff1)
    x, ctx_1024, mask_BxS2_ff1 = _rec_inputs()

    def _L0_attn_setup():
        import jax, jax.numpy as jnp
        import numpy as np
        B, N, C, H = (2, 256, 128, 16)
        HD = C // H
        key = jax.random.key(seed)
        k1, k2, k3, k4 = jax.random.split(key, 4)
        s = 1.0 / np.sqrt(C)
        return {'x': jax.random.normal(k1, (B, N, C), dtype=jnp.float32), 'w_qkv': jax.random.normal(k2, (C, 3 * C), dtype=jnp.float32) * s, 'w_proj': jax.random.normal(k3, (C, C), dtype=jnp.float32) * s, 'b_proj': jax.random.normal(k4, (C,), dtype=jnp.float32) * 0.02}
    _L0_attn_all = _L0_attn_setup()
    _L0_attn_in = {k: v for k, v in _L0_attn_all.items() if k in ('w_qkv', 'w_proj', 'b_proj')}
    del _L0_attn_all

    def _L0_xattn_setup():
        import jax, jax.numpy as jnp
        import numpy as np
        D_MODEL = 128
        NUM_HEADS = 16
        HEAD_DIM = D_MODEL // NUM_HEADS
        MAX_SEQ = 64

        def rope_tables(seq_len, dim):
            inv_freq = 1.0 / 10000.0 ** (jnp.arange(0, dim, 2, dtype=jnp.float32) / dim)
            t = jnp.arange(seq_len, dtype=jnp.float32)
            freqs = jnp.einsum('i,j->ij', t, inv_freq)
            emb = jnp.concatenate([freqs, freqs], axis=-1)
            return (jnp.cos(emb), jnp.sin(emb))

        def rotate_half(x):
            x1, x2 = jnp.split(x, 2, axis=-1)
            return jnp.concatenate([-x2, x1], axis=-1)
        key = jax.random.key(seed)
        ks = jax.random.split(key, 12)
        B, S, D = (16, 64, D_MODEL)
        s = 1.0 / np.sqrt(D)
        inp = {'query': jax.random.normal(ks[0], (B, S, D), jnp.float32), 'key': jax.random.normal(ks[1], (B, S, D), jnp.float32), 'value': jax.random.normal(ks[2], (B, S, D), jnp.float32), 'Wq': jax.random.normal(ks[3], (D, D), jnp.float32) * s, 'bq': jnp.zeros((D,), jnp.float32), 'Wk': jax.random.normal(ks[4], (D, D), jnp.float32) * s, 'bk': jnp.zeros((D,), jnp.float32), 'Wv': jax.random.normal(ks[5], (D, D), jnp.float32) * s, 'bv': jnp.zeros((D,), jnp.float32), 'Wo': jax.random.normal(ks[6], (D, D), jnp.float32) * s, 'bo': jnp.zeros((D,), jnp.float32)}
        return inp
    _L0_xattn_all = _L0_xattn_setup()
    _L0_xattn_in = {k: v for k, v in _L0_xattn_all.items() if k in ('Wq', 'bq', 'Wk', 'bk', 'Wv', 'bv', 'Wo', 'bo')}
    del _L0_xattn_all

    def _L0_ffn_setup():
        import jax, jax.numpy as jnp
        import numpy as np
        D_MODEL = 128
        D_FF = 512
        N_ZONES = 8
        TOP_K = 3
        ROUTER_H = 32
        BATCH = 16
        SEQ = 256
        key = jax.random.key(seed)
        ks = jax.random.split(key, 8)
        s = lambda *dims: 1.0 / np.sqrt(dims[-2] if len(dims) > 1 else dims[-1])
        x = jax.random.normal(ks[0], (BATCH, SEQ, D_MODEL), dtype=jnp.float32)
        W1 = jax.random.normal(ks[1], (D_MODEL, ROUTER_H), dtype=jnp.float32) / np.sqrt(D_MODEL)
        b1 = jnp.zeros((ROUTER_H,), dtype=jnp.float32)
        W2 = jax.random.normal(ks[2], (ROUTER_H, N_ZONES), dtype=jnp.float32) / np.sqrt(ROUTER_H)
        b2 = jnp.zeros((N_ZONES,), dtype=jnp.float32)
        Wa = jax.random.normal(ks[3], (N_ZONES, D_MODEL, D_FF), dtype=jnp.float32) / np.sqrt(D_MODEL)
        Wb = jax.random.normal(ks[4], (N_ZONES, D_FF, D_MODEL), dtype=jnp.float32) / np.sqrt(D_FF)
        return {'x': x, 'W1': W1, 'b1': b1, 'W2': W2, 'b2': b2, 'Wa': Wa, 'Wb': Wb}
    _L0_ffn_all = _L0_ffn_setup()
    _L0_ffn_in = {k: v for k, v in _L0_ffn_all.items() if k in ('W1', 'b1', 'W2', 'b2', 'Wa', 'Wb')}
    del _L0_ffn_all

    def _L1_attn_setup():
        import jax, jax.numpy as jnp
        import numpy as np
        D_MODEL = 128
        D_HEAD = 64
        N_HEADS = 16
        STATE = 64
        D_INNER = D_HEAD * N_HEADS
        B, T = (4, 256)
        LN_EPS = 1e-05

        def _linear_params(key, fan_out, fan_in):
            k1, k2 = jax.random.split(key)
            s = 1.0 / np.sqrt(fan_in)
            W = jax.random.uniform(k1, (fan_out, fan_in), jnp.float32, -s, s)
            b = jax.random.uniform(k2, (fan_out,), jnp.float32, -s, s)
            return (W, b)

        def _layer_norm(x, gamma, beta):
            mu = jnp.mean(x, axis=-1, keepdims=True)
            var = jnp.mean(jnp.square(x - mu), axis=-1, keepdims=True)
            return (x - mu) * jax.lax.rsqrt(var + LN_EPS) * gamma + beta
        key = jax.random.key(seed)
        ks = jax.random.split(key, 8)
        WQ, bQ = _linear_params(ks[0], D_INNER, D_MODEL)
        WK, bK = _linear_params(ks[1], D_INNER, D_MODEL)
        WV, bV = _linear_params(ks[2], D_INNER, D_MODEL)
        WO, bO = _linear_params(ks[3], D_MODEL, D_INNER)
        Wg, bg = _linear_params(ks[4], D_INNER, D_MODEL)
        alpha_logit = jax.random.normal(ks[5], (N_HEADS, STATE), jnp.float32) * 0.1
        ln_gamma = jnp.ones((D_MODEL,), jnp.float32)
        ln_beta = jnp.zeros((D_MODEL,), jnp.float32)
        x = jax.random.normal(ks[6], (B, T, D_MODEL), jnp.float32)
        return {'x': x, 'WQ': WQ, 'bQ': bQ, 'WK': WK, 'bK': bK, 'WV': WV, 'bV': bV, 'WO': WO, 'bO': bO, 'Wg': Wg, 'bg': bg, 'alpha_logit': alpha_logit, 'ln_gamma': ln_gamma, 'ln_beta': ln_beta}
    _L1_attn_all = _L1_attn_setup()
    _L1_attn_in = {k: v for k, v in _L1_attn_all.items() if k in ('WQ', 'bQ', 'WK', 'bK', 'WV', 'bV', 'WO', 'bO', 'Wg', 'bg', 'alpha_logit', 'ln_gamma', 'ln_beta')}
    del _L1_attn_all

    def _L1_xattn_setup():
        import jax, jax.numpy as jnp
        import numpy as np
        HEADS = 16
        LARGE_BIAS = 10000.0
        key = jax.random.key(seed)
        k1, k2, k3, k4 = jax.random.split(key, 4)
        B, S, D = (2, 256, 128)
        query = jax.random.normal(k1, (B, S, D), dtype=jnp.float32)
        key_t = jax.random.normal(k2, (B, S, D), dtype=jnp.float32)
        value = jax.random.normal(k3, (B, S, D), dtype=jnp.float32)
        mask = jnp.ones((B, S), dtype=jnp.float32)
        limit = np.sqrt(6.0 / (D + D)).astype(np.float32)
        W_o = jax.random.uniform(k4, (D, D), dtype=jnp.float32, minval=-limit, maxval=limit)
        return {'query': query, 'key': key_t, 'value': value, 'mask': mask, 'W_o': W_o}
    _L1_xattn_all = _L1_xattn_setup()
    _L1_xattn_in = {k: v for k, v in _L1_xattn_all.items() if k in ('W_o',)}
    del _L1_xattn_all

    def _L1_ffn_setup():
        import jax, jax.numpy as jnp
        import numpy as np
        H = 128
        I = 256
        E = 8
        B, S = (2, 128)

        def _swiglu(x, wg, wu, wd):
            return jax.nn.silu(x @ wg) * (x @ wu) @ wd
        key = jax.random.key(seed)
        ks = jax.random.split(key, 8)
        sc_h = 1.0 / np.sqrt(H)
        sc_i = 1.0 / np.sqrt(I)
        return {'hidden_states': jax.random.normal(ks[0], (B, S, H), jnp.float32), 'gate_w': jax.random.normal(ks[1], (H, E), jnp.float32) * sc_h, 'sh_gate': jax.random.normal(ks[2], (H, I), jnp.float32) * sc_h, 'sh_up': jax.random.normal(ks[3], (H, I), jnp.float32) * sc_h, 'sh_down': jax.random.normal(ks[4], (I, H), jnp.float32) * sc_i, 'rt_gate': jax.random.normal(ks[5], (E, H, I), jnp.float32) * sc_h, 'rt_up': jax.random.normal(ks[6], (E, H, I), jnp.float32) * sc_h, 'rt_down': jax.random.normal(ks[7], (E, I, H), jnp.float32) * sc_i}
    _L1_ffn_all = _L1_ffn_setup()
    _L1_ffn_in = {k: v for k, v in _L1_ffn_all.items() if k in ('gate_w', 'sh_gate', 'sh_up', 'sh_down', 'rt_gate', 'rt_up', 'rt_down')}
    del _L1_ffn_all

    def _L2_attn_setup():
        import jax, jax.numpy as jnp
        import numpy as np
        HID = 128
        DIN = 256
        N = 16
        DTR = 64
        TW = 4

        def _causal_conv(xc, w_conv, b_conv):
            b, l, d = xc.shape
            xp = jnp.pad(xc, ((0, 0), (TW - 1, 0), (0, 0)))
            y = b_conv
            for k in range(TW):
                y = y + xp[:, k:k + l, :] * w_conv[k]
            return y

        def _forward(x, w_in, b_in, w_conv, b_conv, w_x, w_dt, A_log, D, w_out):
            b, l, _ = x.shape
            xr = x @ w_in + b_in
            xc, res = jnp.split(xr, 2, axis=-1)
            u = jax.nn.silu(_causal_conv(xc, w_conv, b_conv))
            A = -jnp.exp(A_log)
            x_dbl = u @ w_x
            dt, B, C = jnp.split(x_dbl, [DTR, DTR + N], axis=-1)
            delta = jax.nn.softplus(dt @ w_dt)
            deltaA = jnp.exp(delta[..., None] * A)
            deltaBu = delta[..., None] * B[:, :, None, :] * u[..., None]

            def step(h, ab):
                a, bu = ab
                h = a * h + bu
                return (h, h)
            a_t = jnp.moveaxis(deltaA, 1, 0)
            bu_t = jnp.moveaxis(deltaBu, 1, 0)
            h0 = jnp.zeros((b, DIN, N), dtype=x.dtype)
            _, hs = jax.lax.scan(step, h0, (a_t, bu_t))
            hs = jnp.moveaxis(hs, 0, 1)
            y = jnp.einsum('bldn,bln->bld', hs, C) + u * D
            return y * jax.nn.silu(res) @ w_out
        key = jax.random.key(seed)
        ks = jax.random.split(key, 10)
        s = lambda *shape: 1.0 / np.sqrt(shape[0])
        x = jax.random.normal(ks[0], (2, 256, HID), dtype=jnp.float32)
        w_in = jax.random.normal(ks[1], (HID, 2 * DIN), dtype=jnp.float32) * s(HID)
        b_in = jax.random.normal(ks[2], (2 * DIN,), dtype=jnp.float32) * 0.02
        w_conv = jax.random.normal(ks[3], (TW, DIN), dtype=jnp.float32) * 0.5
        b_conv = jax.random.normal(ks[4], (DIN,), dtype=jnp.float32) * 0.02
        w_x = jax.random.normal(ks[5], (DIN, DTR + 2 * N), dtype=jnp.float32) * s(DIN)
        w_dt = jax.random.normal(ks[6], (DTR, DIN), dtype=jnp.float32) * s(DTR)
        A_log = jnp.log(jnp.broadcast_to(jnp.arange(1, N + 1, dtype=jnp.float32), (DIN, N)))
        D = jnp.ones((DIN,), dtype=jnp.float32)
        w_out = jax.random.normal(ks[7], (DIN, HID), dtype=jnp.float32) * s(DIN)
        return {'x': x, 'w_in': w_in, 'b_in': b_in, 'w_conv': w_conv, 'b_conv': b_conv, 'w_x': w_x, 'w_dt': w_dt, 'A_log': A_log, 'D': D, 'w_out': w_out}
    _L2_attn_all = _L2_attn_setup()
    _L2_attn_in = {k: v for k, v in _L2_attn_all.items() if k in ('w_in', 'b_in', 'w_conv', 'b_conv', 'w_x', 'w_dt', 'A_log', 'D', 'w_out')}
    del _L2_attn_all

    def _L2_xattn_setup():
        import jax, jax.numpy as jnp
        import numpy as np
        H = 128
        B = 8
        L_CHAR = 256
        L_SUB = 128

        def _linear(x, W, b):
            return jnp.einsum('blh,oh->blo', x, W) + b

        def _interp_linear(x, out_len):
            L_in = x.shape[1]
            pos = (jnp.arange(out_len, dtype=x.dtype) + 0.5) * (L_in / out_len) - 0.5
            pos = jnp.clip(pos, 0.0, L_in - 1)
            lo = jnp.floor(pos).astype(jnp.int32)
            hi = jnp.minimum(lo + 1, L_in - 1)
            w = (pos - lo.astype(x.dtype))[None, :, None]
            return x[:, lo] * (1 - w) + x[:, hi] * w
        key = jax.random.key(seed)
        ks = jax.random.split(key, 18)
        s = 0.02
        inp = {'char_emb': jax.random.normal(ks[0], (B, L_CHAR, H), jnp.float32), 'subword_emb': jax.random.normal(ks[1], (B, L_SUB, H), jnp.float32)}
        names = ['Wq_c', 'Wk_s', 'Wv_s', 'Wq_s', 'Wk_c', 'Wv_c']
        for i, n in enumerate(names):
            inp[n] = jax.random.normal(ks[2 + 2 * i], (H, H), jnp.float32) * s
            inp['b' + n[1:]] = jax.random.normal(ks[3 + 2 * i], (H,), jnp.float32) * s
        inp['Wg'] = jax.random.normal(ks[14], (H, 2 * H), jnp.float32) * s
        inp['bg'] = jax.random.normal(ks[15], (H,), jnp.float32) * s
        return inp
    _L2_xattn_all = _L2_xattn_setup()
    _L2_xattn_in = {k: v for k, v in _L2_xattn_all.items() if k in ('Wq_c', 'bq_c', 'Wk_s', 'bk_s', 'Wv_s', 'bv_s', 'Wq_s', 'bq_s', 'Wk_c', 'bk_c', 'Wv_c', 'bv_c', 'Wg', 'bg')}
    del _L2_xattn_all

    def _L2_ffn_setup():
        import jax, jax.numpy as jnp
        import numpy as np
        LN_EPS = 0.001
        EPS = 1e-05
        QB = 128.0

        def ste_round(x):
            return x + jax.lax.stop_gradient(jnp.round(x) - x)
        key = jax.random.key(seed)
        k1, k2 = jax.random.split(key)
        x = jax.random.normal(k1, (4, 1024, 128), dtype=jnp.float32)
        weight = jax.random.normal(k2, (128, 128), dtype=jnp.float32) * 0.02
        ln_gamma = jnp.ones((128,), dtype=jnp.float32)
        ln_beta = jnp.zeros((128,), dtype=jnp.float32)
        return {'x': x, 'weight': weight, 'ln_gamma': ln_gamma, 'ln_beta': ln_beta}
    _L2_ffn_all = _L2_ffn_setup()
    _L2_ffn_in = {k: v for k, v in _L2_ffn_all.items() if k in ('weight', 'ln_gamma', 'ln_beta')}
    del _L2_ffn_all

    def _L3_attn_setup():
        import jax, jax.numpy as jnp
        import numpy as np
        N_EMBD = 128
        N_HEAD = 16
        N_LAYER = 24
        LAYER_ID = 12
        B, T = (4, 512)
        Q = 64
        EPS = 1e-05 * 64

        def _static_params():
            C, H = (N_EMBD, N_HEAD)
            r01 = LAYER_ID / (N_LAYER - 1)
            r1a0 = 1.0 - LAYER_ID / N_LAYER
            ddd = np.arange(C, dtype=np.float64) / C
            maa_k = (1.0 - ddd ** r1a0).astype(np.float32).reshape(1, 1, C)
            maa_v = (1.0 - (ddd ** r1a0 + 0.3 * r01)).astype(np.float32).reshape(1, 1, C)
            maa_r = (1.0 - ddd ** (0.5 * r1a0)).astype(np.float32).reshape(1, 1, C)
            maa_g = maa_r.copy()
            h = np.arange(H, dtype=np.float64)
            decay = (-6.0 + 5.0 * (h / (H - 1)) ** (0.7 + 1.3 * r01)).astype(np.float32).reshape(H, 1)
            faaaa = (r01 * (1.0 - h / (H - 1))).astype(np.float32).reshape(H, 1)
            return (maa_k, maa_v, maa_r, maa_g, decay, faaaa)

        def _rwkv_forward(x, time_maa_k, time_maa_v, time_maa_r, time_maa_g, time_decay, time_faaaa, Wr, Wk, Wv, Wg, Wo, ln_w, ln_b):
            Bv, Tv, C = x.shape
            H = N_HEAD
            N = C // H
            nC = Tv // Q
            xx = jnp.pad(x, ((0, 0), (1, 0), (0, 0)))[:, :Tv] - x
            xk = x + xx * time_maa_k
            xv = x + xx * time_maa_v
            xr = x + xx * time_maa_r
            xg = x + xx * time_maa_g
            r = (xr @ Wr.T).reshape(Bv, Tv, H, N).transpose(0, 2, 1, 3)
            k = (xk @ Wk.T).reshape(Bv, Tv, H, N).transpose(0, 2, 3, 1)
            v = (xv @ Wv.T).reshape(Bv, Tv, H, N).transpose(0, 2, 1, 3)
            g = jax.nn.gelu(xg @ Wg.T, approximate=False)
            w = jnp.exp(-jnp.exp(time_decay))[:, 0]
            u = time_faaaa[:, 0]
            q = jnp.arange(Q)
            ws = (w ** Q).reshape(1, H, 1, 1)
            wk = (w[:, None] ** (Q - 1 - q)).reshape(1, H, 1, Q)
            wb = (w[:, None] ** q).reshape(1, H, Q, 1)
            i_idx = q[:, None]
            j_idx = q[None, :]
            e = jnp.maximum(i_idx - j_idx - 1, 0)
            Wmat = jnp.where(i_idx > j_idx, w[:, None, None] ** e, 0.0)
            Wmat = Wmat + jnp.eye(Q, dtype=x.dtype) * u[:, None, None]
            Wmat = Wmat.reshape(1, H, Q, Q)
            rr = r.reshape(Bv, H, nC, Q, N).transpose(2, 0, 1, 3, 4)
            kk = k.reshape(Bv, H, N, nC, Q).transpose(3, 0, 1, 2, 4)
            vv = v.reshape(Bv, H, nC, Q, N).transpose(2, 0, 1, 3, 4)

            def step(state, inp):
                rc, kc, vc = inp
                att = rc @ kc
                yc = att * Wmat @ vc + rc @ state * wb
                new_state = ws * state + kc * wk @ vc
                return (new_state, yc)
            state0 = jnp.zeros((Bv, H, N, N), dtype=x.dtype)
            _, ys = jax.lax.scan(step, state0, (rr, kk, vv))
            y = ys.transpose(1, 2, 0, 3, 4).reshape(Bv, H, Tv, N)
            y = y.transpose(0, 2, 1, 3)
            mean = y.mean(axis=-1, keepdims=True)
            var = y.var(axis=-1, keepdims=True)
            yn = (y - mean) / jnp.sqrt(var + EPS)
            yn = yn * ln_w.reshape(1, 1, H, N) + ln_b.reshape(1, 1, H, N)
            yn = yn.reshape(Bv, Tv, C)
            out = yn * g @ Wo.T
            return out
        key = jax.random.key(seed)
        ks = jax.random.split(key, 8)
        C = N_EMBD
        maa_k, maa_v, maa_r, maa_g, decay, faaaa = _static_params()
        std = 0.02
        return {'x': jax.random.normal(ks[0], (B, T, C), dtype=jnp.float32), 'time_maa_k': jnp.asarray(maa_k), 'time_maa_v': jnp.asarray(maa_v), 'time_maa_r': jnp.asarray(maa_r), 'time_maa_g': jnp.asarray(maa_g), 'time_decay': jnp.asarray(decay), 'time_faaaa': jnp.asarray(faaaa), 'Wr': jax.random.normal(ks[1], (C, C), dtype=jnp.float32) * std, 'Wk': jax.random.normal(ks[2], (C, C), dtype=jnp.float32) * std, 'Wv': jax.random.normal(ks[3], (C, C), dtype=jnp.float32) * std, 'Wg': jax.random.normal(ks[4], (C, C), dtype=jnp.float32) * std, 'Wo': jax.random.normal(ks[5], (C, C), dtype=jnp.float32) * std, 'ln_w': jnp.ones((C,), dtype=jnp.float32), 'ln_b': jnp.zeros((C,), dtype=jnp.float32)}
    _L3_attn_all = _L3_attn_setup()
    _L3_attn_in = {k: v for k, v in _L3_attn_all.items() if k in ('time_maa_k', 'time_maa_v', 'time_maa_r', 'time_maa_g', 'time_decay', 'time_faaaa', 'Wr', 'Wk', 'Wv', 'Wg', 'Wo', 'ln_w', 'ln_b')}
    del _L3_attn_all

    def _L3_xattn_setup():
        import jax, jax.numpy as jnp
        import numpy as np
        DIM = 128
        HEADS = 16
        DIM_HEAD = 64
        INNER = HEADS * DIM_HEAD
        MLP = 512
        EPS = 1e-05

        def _layernorm(x, g, b):
            mu = jnp.mean(x, axis=-1, keepdims=True)
            var = jnp.mean(jnp.square(x - mu), axis=-1, keepdims=True)
            return (x - mu) * jax.lax.rsqrt(var + EPS) * g + b

        def _l2norm(x):
            n = jnp.sqrt(jnp.sum(jnp.square(x), axis=-1, keepdims=True))
            return x / jnp.maximum(n, 1e-12)

        def _split_heads(x, B, N):
            return x.reshape(B, N, HEADS, DIM_HEAD).transpose(0, 2, 1, 3)
        key = jax.random.key(seed)
        ks = jax.random.split(key, 16)
        B, N = (4, 256)
        s = 0.02
        return {'Q': jax.random.normal(ks[0], (B, N, DIM), jnp.float32), 'K': jax.random.normal(ks[1], (B, N, DIM), jnp.float32), 'V': jax.random.normal(ks[2], (B, N, DIM), jnp.float32), 'wq': jax.random.normal(ks[3], (DIM, INNER), jnp.float32) * s, 'wk': jax.random.normal(ks[4], (DIM, INNER), jnp.float32) * s, 'wv': jax.random.normal(ks[5], (DIM, INNER), jnp.float32) * s, 'wo': jax.random.normal(ks[6], (INNER, DIM), jnp.float32) * s, 'bo': jnp.zeros((DIM,), jnp.float32), 'w1': jax.random.normal(ks[7], (DIM, MLP), jnp.float32) * s, 'b1': jnp.zeros((MLP,), jnp.float32), 'w2': jax.random.normal(ks[8], (MLP, DIM), jnp.float32) * s, 'b2': jnp.zeros((DIM,), jnp.float32), 'ln1_g': jnp.ones((DIM,), jnp.float32), 'ln1_b': jnp.zeros((DIM,), jnp.float32), 'ln2_g': jnp.ones((DIM,), jnp.float32), 'ln2_b': jnp.zeros((DIM,), jnp.float32)}
    _L3_xattn_all = _L3_xattn_setup()
    _L3_xattn_in = {k: v for k, v in _L3_xattn_all.items() if k in ('wq', 'wk', 'wv', 'wo', 'bo', 'w1', 'b1', 'w2', 'b2', 'ln1_g', 'ln1_b', 'ln2_g', 'ln2_b')}
    del _L3_xattn_all

    def _L3_ffn_setup():
        import jax, jax.numpy as jnp
        import numpy as np
        TOP_K = 2
        TEMP = 0.9
        EPS = 1e-05
        B, S, D, F, E = (2, 256, 128, 512, 8)

        def _moe_forward(x, gate_w, gate_b, w1, b1, w2, b2, ln_g, ln_b):
            logits = (x @ gate_w + gate_b) / TEMP
            topk_vals, topk_idx = jax.lax.top_k(logits, TOP_K)
            keep = jax.nn.one_hot(topk_idx, E, dtype=jnp.bool_).any(-2)
            masked = jnp.where(keep, logits, -jnp.inf)
            gate_probs = jax.nn.softmax(masked, axis=-1)
            h = jnp.einsum('bsd,edf->bsef', x, w1) + b1
            h = jax.nn.gelu(h, approximate=False)
            expert_out = jnp.einsum('bsef,efd->bsed', h, w2) + b2
            out = jnp.einsum('bse,bsed->bsd', gate_probs, expert_out)
            mu = out.mean(-1, keepdims=True)
            var = out.var(-1, keepdims=True)
            out = (out - mu) / jnp.sqrt(var + EPS) * ln_g + ln_b
            return out
        key = jax.random.key(seed)
        ks = jax.random.split(key, 4)
        scale_in = 1.0 / np.sqrt(D)
        scale_ff = 1.0 / np.sqrt(F)
        return {'x': jax.random.normal(ks[0], (B, S, D), jnp.float32), 'gate_w': jax.random.normal(ks[1], (D, E), jnp.float32) * scale_in, 'gate_b': jnp.zeros((E,), jnp.float32), 'w1': jax.random.normal(ks[2], (E, D, F), jnp.float32) * scale_in, 'b1': jnp.zeros((E, F), jnp.float32), 'w2': jax.random.normal(ks[3], (E, F, D), jnp.float32) * scale_ff, 'b2': jnp.zeros((E, D), jnp.float32), 'ln_g': jnp.ones((D,), jnp.float32), 'ln_b': jnp.zeros((D,), jnp.float32)}
    _L3_ffn_all = _L3_ffn_setup()
    _L3_ffn_in = {k: v for k, v in _L3_ffn_all.items() if k in ('gate_w', 'gate_b', 'w1', 'b1', 'w2', 'b2', 'ln_g', 'ln_b')}
    del _L3_ffn_all
    return {'x': x, 'ctx_1024': ctx_1024, 'mask_BxS2_ff1': mask_BxS2_ff1, 'L0_attn_w_qkv': _L0_attn_in['w_qkv'], 'L0_attn_w_proj': _L0_attn_in['w_proj'], 'L0_attn_b_proj': _L0_attn_in['b_proj'], 'L0_xattn_Wq': _L0_xattn_in['Wq'], 'L0_xattn_bq': _L0_xattn_in['bq'], 'L0_xattn_Wk': _L0_xattn_in['Wk'], 'L0_xattn_bk': _L0_xattn_in['bk'], 'L0_xattn_Wv': _L0_xattn_in['Wv'], 'L0_xattn_bv': _L0_xattn_in['bv'], 'L0_xattn_Wo': _L0_xattn_in['Wo'], 'L0_xattn_bo': _L0_xattn_in['bo'], 'L0_ffn_W1': _L0_ffn_in['W1'], 'L0_ffn_b1': _L0_ffn_in['b1'], 'L0_ffn_W2': _L0_ffn_in['W2'], 'L0_ffn_b2': _L0_ffn_in['b2'], 'L0_ffn_Wa': _L0_ffn_in['Wa'], 'L0_ffn_Wb': _L0_ffn_in['Wb'], 'L1_attn_WQ': _L1_attn_in['WQ'], 'L1_attn_bQ': _L1_attn_in['bQ'], 'L1_attn_WK': _L1_attn_in['WK'], 'L1_attn_bK': _L1_attn_in['bK'], 'L1_attn_WV': _L1_attn_in['WV'], 'L1_attn_bV': _L1_attn_in['bV'], 'L1_attn_WO': _L1_attn_in['WO'], 'L1_attn_bO': _L1_attn_in['bO'], 'L1_attn_Wg': _L1_attn_in['Wg'], 'L1_attn_bg': _L1_attn_in['bg'], 'L1_attn_alpha_logit': _L1_attn_in['alpha_logit'], 'L1_attn_ln_gamma': _L1_attn_in['ln_gamma'], 'L1_attn_ln_beta': _L1_attn_in['ln_beta'], 'L1_xattn_W_o': _L1_xattn_in['W_o'], 'L1_ffn_gate_w': _L1_ffn_in['gate_w'], 'L1_ffn_sh_gate': _L1_ffn_in['sh_gate'], 'L1_ffn_sh_up': _L1_ffn_in['sh_up'], 'L1_ffn_sh_down': _L1_ffn_in['sh_down'], 'L1_ffn_rt_gate': _L1_ffn_in['rt_gate'], 'L1_ffn_rt_up': _L1_ffn_in['rt_up'], 'L1_ffn_rt_down': _L1_ffn_in['rt_down'], 'L2_attn_w_in': _L2_attn_in['w_in'], 'L2_attn_b_in': _L2_attn_in['b_in'], 'L2_attn_w_conv': _L2_attn_in['w_conv'], 'L2_attn_b_conv': _L2_attn_in['b_conv'], 'L2_attn_w_x': _L2_attn_in['w_x'], 'L2_attn_w_dt': _L2_attn_in['w_dt'], 'L2_attn_A_log': _L2_attn_in['A_log'], 'L2_attn_D': _L2_attn_in['D'], 'L2_attn_w_out': _L2_attn_in['w_out'], 'L2_xattn_Wq_c': _L2_xattn_in['Wq_c'], 'L2_xattn_bq_c': _L2_xattn_in['bq_c'], 'L2_xattn_Wk_s': _L2_xattn_in['Wk_s'], 'L2_xattn_bk_s': _L2_xattn_in['bk_s'], 'L2_xattn_Wv_s': _L2_xattn_in['Wv_s'], 'L2_xattn_bv_s': _L2_xattn_in['bv_s'], 'L2_xattn_Wq_s': _L2_xattn_in['Wq_s'], 'L2_xattn_bq_s': _L2_xattn_in['bq_s'], 'L2_xattn_Wk_c': _L2_xattn_in['Wk_c'], 'L2_xattn_bk_c': _L2_xattn_in['bk_c'], 'L2_xattn_Wv_c': _L2_xattn_in['Wv_c'], 'L2_xattn_bv_c': _L2_xattn_in['bv_c'], 'L2_xattn_Wg': _L2_xattn_in['Wg'], 'L2_xattn_bg': _L2_xattn_in['bg'], 'L2_ffn_weight': _L2_ffn_in['weight'], 'L2_ffn_ln_gamma': _L2_ffn_in['ln_gamma'], 'L2_ffn_ln_beta': _L2_ffn_in['ln_beta'], 'L3_attn_time_maa_k': _L3_attn_in['time_maa_k'], 'L3_attn_time_maa_v': _L3_attn_in['time_maa_v'], 'L3_attn_time_maa_r': _L3_attn_in['time_maa_r'], 'L3_attn_time_maa_g': _L3_attn_in['time_maa_g'], 'L3_attn_time_decay': _L3_attn_in['time_decay'], 'L3_attn_time_faaaa': _L3_attn_in['time_faaaa'], 'L3_attn_Wr': _L3_attn_in['Wr'], 'L3_attn_Wk': _L3_attn_in['Wk'], 'L3_attn_Wv': _L3_attn_in['Wv'], 'L3_attn_Wg': _L3_attn_in['Wg'], 'L3_attn_Wo': _L3_attn_in['Wo'], 'L3_attn_ln_w': _L3_attn_in['ln_w'], 'L3_attn_ln_b': _L3_attn_in['ln_b'], 'L3_xattn_wq': _L3_xattn_in['wq'], 'L3_xattn_wk': _L3_xattn_in['wk'], 'L3_xattn_wv': _L3_xattn_in['wv'], 'L3_xattn_wo': _L3_xattn_in['wo'], 'L3_xattn_bo': _L3_xattn_in['bo'], 'L3_xattn_w1': _L3_xattn_in['w1'], 'L3_xattn_b1': _L3_xattn_in['b1'], 'L3_xattn_w2': _L3_xattn_in['w2'], 'L3_xattn_b2': _L3_xattn_in['b2'], 'L3_xattn_ln1_g': _L3_xattn_in['ln1_g'], 'L3_xattn_ln1_b': _L3_xattn_in['ln1_b'], 'L3_xattn_ln2_g': _L3_xattn_in['ln2_g'], 'L3_xattn_ln2_b': _L3_xattn_in['ln2_b'], 'L3_ffn_gate_w': _L3_ffn_in['gate_w'], 'L3_ffn_gate_b': _L3_ffn_in['gate_b'], 'L3_ffn_w1': _L3_ffn_in['w1'], 'L3_ffn_b1': _L3_ffn_in['b1'], 'L3_ffn_w2': _L3_ffn_in['w2'], 'L3_ffn_b2': _L3_ffn_in['b2'], 'L3_ffn_ln_g': _L3_ffn_in['ln_g'], 'L3_ffn_ln_b': _L3_ffn_in['ln_b']}

def reference(x, ctx_1024, mask_BxS2_ff1, L0_attn_w_qkv, L0_attn_w_proj, L0_attn_b_proj, L0_xattn_Wq, L0_xattn_bq, L0_xattn_Wk, L0_xattn_bk, L0_xattn_Wv, L0_xattn_bv, L0_xattn_Wo, L0_xattn_bo, L0_ffn_W1, L0_ffn_b1, L0_ffn_W2, L0_ffn_b2, L0_ffn_Wa, L0_ffn_Wb, L1_attn_WQ, L1_attn_bQ, L1_attn_WK, L1_attn_bK, L1_attn_WV, L1_attn_bV, L1_attn_WO, L1_attn_bO, L1_attn_Wg, L1_attn_bg, L1_attn_alpha_logit, L1_attn_ln_gamma, L1_attn_ln_beta, L1_xattn_W_o, L1_ffn_gate_w, L1_ffn_sh_gate, L1_ffn_sh_up, L1_ffn_sh_down, L1_ffn_rt_gate, L1_ffn_rt_up, L1_ffn_rt_down, L2_attn_w_in, L2_attn_b_in, L2_attn_w_conv, L2_attn_b_conv, L2_attn_w_x, L2_attn_w_dt, L2_attn_A_log, L2_attn_D, L2_attn_w_out, L2_xattn_Wq_c, L2_xattn_bq_c, L2_xattn_Wk_s, L2_xattn_bk_s, L2_xattn_Wv_s, L2_xattn_bv_s, L2_xattn_Wq_s, L2_xattn_bq_s, L2_xattn_Wk_c, L2_xattn_bk_c, L2_xattn_Wv_c, L2_xattn_bv_c, L2_xattn_Wg, L2_xattn_bg, L2_ffn_weight, L2_ffn_ln_gamma, L2_ffn_ln_beta, L3_attn_time_maa_k, L3_attn_time_maa_v, L3_attn_time_maa_r, L3_attn_time_maa_g, L3_attn_time_decay, L3_attn_time_faaaa, L3_attn_Wr, L3_attn_Wk, L3_attn_Wv, L3_attn_Wg, L3_attn_Wo, L3_attn_ln_w, L3_attn_ln_b, L3_xattn_wq, L3_xattn_wk, L3_xattn_wv, L3_xattn_wo, L3_xattn_bo, L3_xattn_w1, L3_xattn_b1, L3_xattn_w2, L3_xattn_b2, L3_xattn_ln1_g, L3_xattn_ln1_b, L3_xattn_ln2_g, L3_xattn_ln2_b, L3_ffn_gate_w, L3_ffn_gate_b, L3_ffn_w1, L3_ffn_b1, L3_ffn_w2, L3_ffn_b2, L3_ffn_ln_g, L3_ffn_ln_b):
    import jax
    import jax.numpy as jnp

    def _L0_attn_ref(x, w_qkv, w_proj, b_proj):
        import jax, jax.numpy as jnp
        import numpy as np
        B, N, C, H = (2, 256, 128, 16)
        HD = C // H
        b, n, c = x.shape
        scale = (c // H) ** (-0.5)
        qkv = (x @ w_qkv).reshape(b, n, 3, H, c // H)
        q = qkv[:, :, 0].transpose(0, 2, 1, 3) * scale
        k = qkv[:, :, 1].transpose(0, 2, 1, 3)
        v = qkv[:, :, 2].transpose(0, 2, 1, 3)
        attn = jnp.einsum('bhqd,bhkd->bhqk', q, k)
        causal = jnp.triu(jnp.ones((n, n), dtype=bool), k=1)
        attn = jnp.where(causal[None, None], -jnp.inf, attn)
        attn = jax.nn.softmax(attn, axis=-1)
        out = jnp.einsum('bhqk,bhkd->bhqd', attn, v)
        out = out.transpose(0, 2, 1, 3).reshape(b, n, c)
        return out @ w_proj + b_proj

    def _L0_xattn_ref(query, key, value, Wq, bq, Wk, bk, Wv, bv, Wo, bo):
        import jax, jax.numpy as jnp
        import numpy as np
        D_MODEL = 128
        NUM_HEADS = 16
        HEAD_DIM = D_MODEL // NUM_HEADS
        MAX_SEQ = 64

        def rope_tables(seq_len, dim):
            inv_freq = 1.0 / 10000.0 ** (jnp.arange(0, dim, 2, dtype=jnp.float32) / dim)
            t = jnp.arange(seq_len, dtype=jnp.float32)
            freqs = jnp.einsum('i,j->ij', t, inv_freq)
            emb = jnp.concatenate([freqs, freqs], axis=-1)
            return (jnp.cos(emb), jnp.sin(emb))

        def rotate_half(x):
            x1, x2 = jnp.split(x, 2, axis=-1)
            return jnp.concatenate([-x2, x1], axis=-1)
        B, S, D = query.shape
        H, Hd = (NUM_HEADS, HEAD_DIM)
        scale = Hd ** (-0.5)

        def proj(x, W, b):
            y = jnp.einsum('bsd,ed->bse', x, W) + b
            return y.reshape(B, S, H, Hd).transpose(0, 2, 1, 3)
        q = proj(query, Wq, bq)
        k = proj(key, Wk, bk)
        v = proj(value, Wv, bv)
        cos, sin = rope_tables(S, Hd)
        cos = cos[None, None]
        sin = sin[None, None]
        q = q * cos + rotate_half(q) * sin
        k = k * cos + rotate_half(k) * sin
        attn = jnp.einsum('bhqd,bhkd->bhqk', q, k) * scale
        attn_w = jax.nn.softmax(attn, axis=-1)
        out = jnp.einsum('bhqk,bhkd->bhqd', attn_w, v)
        out = out.transpose(0, 2, 1, 3).reshape(B, S, D)
        out = jnp.einsum('bsd,ed->bse', out, Wo) + bo
        return out

    def _L0_ffn_ref(x, W1, b1, W2, b2, Wa, Wb):
        import jax, jax.numpy as jnp
        import numpy as np
        D_MODEL = 128
        D_FF = 512
        N_ZONES = 8
        TOP_K = 3
        ROUTER_H = 32
        BATCH = 16
        SEQ = 256
        pooled = x.mean(axis=1)
        h = jnp.tanh(pooled @ W1 + b1)
        logits = h @ W2 + b2
        probs = jax.nn.softmax(logits, axis=-1)
        top_p, top_i = jax.lax.top_k(probs, TOP_K)
        top_w = top_p / top_p.sum(axis=-1, keepdims=True)
        onehot = jax.nn.one_hot(top_i, N_ZONES, dtype=x.dtype)
        w = jnp.einsum('bk,bke->be', top_w, onehot)
        zone_outputs = jnp.zeros_like(x)
        for e in range(N_ZONES):
            z = jax.nn.gelu(x @ Wa[e]) @ Wb[e]
            zone_outputs = zone_outputs + z * w[:, e, None, None]
        return x + zone_outputs

    def _L1_attn_ref(x, WQ, bQ, WK, bK, WV, bV, WO, bO, Wg, bg, alpha_logit, ln_gamma, ln_beta):
        import jax, jax.numpy as jnp
        import numpy as np
        D_MODEL = 128
        D_HEAD = 64
        N_HEADS = 16
        STATE = 64
        D_INNER = D_HEAD * N_HEADS
        B, T = (4, 256)
        LN_EPS = 1e-05

        def _linear_params(key, fan_out, fan_in):
            k1, k2 = jax.random.split(key)
            s = 1.0 / np.sqrt(fan_in)
            W = jax.random.uniform(k1, (fan_out, fan_in), jnp.float32, -s, s)
            b = jax.random.uniform(k2, (fan_out,), jnp.float32, -s, s)
            return (W, b)

        def _layer_norm(x, gamma, beta):
            mu = jnp.mean(x, axis=-1, keepdims=True)
            var = jnp.mean(jnp.square(x - mu), axis=-1, keepdims=True)
            return (x - mu) * jax.lax.rsqrt(var + LN_EPS) * gamma + beta
        batch, seq_len, _ = x.shape
        residual = x
        xn = _layer_norm(x, ln_gamma, ln_beta)
        Q = (xn @ WQ.T + bQ).reshape(batch, seq_len, N_HEADS, D_HEAD)
        K = (xn @ WK.T + bK).reshape(batch, seq_len, N_HEADS, D_HEAD)
        V = (xn @ WV.T + bV).reshape(batch, seq_len, N_HEADS, D_HEAD)
        gate = jax.nn.silu(xn @ Wg.T + bg).reshape(batch, seq_len, N_HEADS, D_HEAD)
        alpha = jax.nn.sigmoid(alpha_logit)
        Qs = Q[..., :STATE]
        Ks = K[..., :STATE]

        def step(h, qkv):
            q, k, v = qkv
            h = alpha[None, :, :, None] * h + k[:, :, :, None] * v[:, :, None, :]
            o = jnp.einsum('bhi,bhij->bhj', q, h)
            return (h, o)
        h0 = jnp.zeros((batch, N_HEADS, STATE, D_HEAD), x.dtype)
        qkv_t = (jnp.moveaxis(Qs, 1, 0), jnp.moveaxis(Ks, 1, 0), jnp.moveaxis(V, 1, 0))
        _, o = jax.lax.scan(step, h0, qkv_t)
        o = jnp.moveaxis(o, 0, 1)
        o = o * gate
        y = o.reshape(batch, seq_len, D_INNER) @ WO.T + bO
        return residual + y

    def _L1_xattn_ref(query, key, value, mask, W_o):
        import jax, jax.numpy as jnp
        import numpy as np
        HEADS = 16
        LARGE_BIAS = 10000.0
        B, S, D = query.shape
        H = HEADS
        U = D // H
        q = query.reshape(B, S, H, U)
        k = key.reshape(B, S, H, U)
        v = value.reshape(B, S, H, U)
        logits = jnp.einsum('bihu,bjhu->bhij', q, k) / jnp.sqrt(jnp.asarray(U, q.dtype))
        bias = (1.0 - mask)[:, None, None, :] * LARGE_BIAS
        weights = jax.nn.softmax(logits - bias, axis=-1)
        attended = jnp.einsum('bhij,bjhu->bihu', weights, v).reshape(B, S, D)
        return attended @ W_o

    def _L1_ffn_ref(hidden_states, gate_w, sh_gate, sh_up, sh_down, rt_gate, rt_up, rt_down):
        import jax, jax.numpy as jnp
        import numpy as np
        H = 128
        I = 256
        E = 8
        B, S = (2, 128)

        def _swiglu(x, wg, wu, wd):
            return jax.nn.silu(x @ wg) * (x @ wu) @ wd
        b, s, h = hidden_states.shape
        x = hidden_states.reshape(-1, h)
        logits = x @ gate_w
        top_val = jnp.max(logits, axis=-1, keepdims=True)
        top_id = jnp.argmax(logits, axis=-1)
        score = jax.nn.sigmoid(top_val)
        xs = x * score
        g = jnp.einsum('th,ehi->eti', xs, rt_gate)
        u = jnp.einsum('th,ehi->eti', xs, rt_up)
        act = jax.nn.silu(g) * u
        y = jnp.einsum('eti,eih->eth', act, rt_down)
        onehot = jax.nn.one_hot(top_id, E, dtype=x.dtype)
        routed = jnp.einsum('eth,te->th', y, onehot)
        shared = _swiglu(x, sh_gate, sh_up, sh_down)
        return (shared + routed).reshape(b, s, h)

    def _L2_attn_ref(x, w_in, b_in, w_conv, b_conv, w_x, w_dt, A_log, D, w_out):
        import jax, jax.numpy as jnp
        import numpy as np
        HID = 128
        DIN = 256
        N = 16
        DTR = 64
        TW = 4

        def _causal_conv(xc, w_conv, b_conv):
            b, l, d = xc.shape
            xp = jnp.pad(xc, ((0, 0), (TW - 1, 0), (0, 0)))
            y = b_conv
            for k in range(TW):
                y = y + xp[:, k:k + l, :] * w_conv[k]
            return y

        def _forward(x, w_in, b_in, w_conv, b_conv, w_x, w_dt, A_log, D, w_out):
            b, l, _ = x.shape
            xr = x @ w_in + b_in
            xc, res = jnp.split(xr, 2, axis=-1)
            u = jax.nn.silu(_causal_conv(xc, w_conv, b_conv))
            A = -jnp.exp(A_log)
            x_dbl = u @ w_x
            dt, B, C = jnp.split(x_dbl, [DTR, DTR + N], axis=-1)
            delta = jax.nn.softplus(dt @ w_dt)
            deltaA = jnp.exp(delta[..., None] * A)
            deltaBu = delta[..., None] * B[:, :, None, :] * u[..., None]

            def step(h, ab):
                a, bu = ab
                h = a * h + bu
                return (h, h)
            a_t = jnp.moveaxis(deltaA, 1, 0)
            bu_t = jnp.moveaxis(deltaBu, 1, 0)
            h0 = jnp.zeros((b, DIN, N), dtype=x.dtype)
            _, hs = jax.lax.scan(step, h0, (a_t, bu_t))
            hs = jnp.moveaxis(hs, 0, 1)
            y = jnp.einsum('bldn,bln->bld', hs, C) + u * D
            return y * jax.nn.silu(res) @ w_out
        return _forward(x, w_in, b_in, w_conv, b_conv, w_x, w_dt, A_log, D, w_out)

    def _L2_xattn_ref(char_emb, subword_emb, Wq_c, bq_c, Wk_s, bk_s, Wv_s, bv_s, Wq_s, bq_s, Wk_c, bk_c, Wv_c, bv_c, Wg, bg):
        import jax, jax.numpy as jnp
        import numpy as np
        H = 128
        B = 8
        L_CHAR = 256
        L_SUB = 128

        def _linear(x, W, b):
            return jnp.einsum('blh,oh->blo', x, W) + b

        def _interp_linear(x, out_len):
            L_in = x.shape[1]
            pos = (jnp.arange(out_len, dtype=x.dtype) + 0.5) * (L_in / out_len) - 0.5
            pos = jnp.clip(pos, 0.0, L_in - 1)
            lo = jnp.floor(pos).astype(jnp.int32)
            hi = jnp.minimum(lo + 1, L_in - 1)
            w = (pos - lo.astype(x.dtype))[None, :, None]
            return x[:, lo] * (1 - w) + x[:, hi] * w
        h = char_emb.shape[-1]
        scale = 1.0 / jnp.sqrt(jnp.asarray(h, char_emb.dtype))
        Q_char = _linear(char_emb, Wq_c, bq_c)
        K_sub = _linear(subword_emb, Wk_s, bk_s)
        V_sub = _linear(subword_emb, Wv_s, bv_s)
        scores = jnp.einsum('bqh,bkh->bqk', Q_char, K_sub) * scale
        char2sub = jnp.einsum('bqk,bkh->bqh', jax.nn.softmax(scores, axis=-1), V_sub)
        Q_sub = _linear(subword_emb, Wq_s, bq_s)
        K_char = _linear(char_emb, Wk_c, bk_c)
        V_char = _linear(char_emb, Wv_c, bv_c)
        scores2 = jnp.einsum('bqh,bkh->bqk', Q_sub, K_char) * scale
        sub2char = jnp.einsum('bqk,bkh->bqh', jax.nn.softmax(scores2, axis=-1), V_char)
        L_char = char_emb.shape[1]
        if sub2char.shape[1] != L_char:
            sub2char = _interp_linear(sub2char, L_char)
        gate_in = jnp.concatenate([char2sub, sub2char], axis=-1)
        gate = jax.nn.sigmoid(jnp.einsum('blh,oh->blo', gate_in, Wg) + bg)
        return gate * char2sub + (1 - gate) * sub2char

    def _L2_ffn_ref(x, weight, ln_gamma, ln_beta):
        import jax, jax.numpy as jnp
        import numpy as np
        LN_EPS = 0.001
        EPS = 1e-05
        QB = 128.0

        def ste_round(x):
            return x + jax.lax.stop_gradient(jnp.round(x) - x)
        mu = jnp.mean(x, axis=-1, keepdims=True)
        var = jnp.var(x, axis=-1, keepdims=True)
        xn = (x - mu) * jax.lax.rsqrt(var + LN_EPS) * ln_gamma + ln_beta
        beta = jnp.mean(jnp.abs(weight))
        w_q = jnp.clip(ste_round(weight / (beta + EPS)), -1.0, 1.0)
        gamma = jnp.max(jnp.abs(xn))
        xq = jnp.clip(xn * QB / gamma, -QB + EPS, QB - EPS)
        y = jnp.einsum('bsd,du->bsu', xq, w_q)
        return y * (gamma * beta / QB)

    def _L3_attn_ref(x, time_maa_k, time_maa_v, time_maa_r, time_maa_g, time_decay, time_faaaa, Wr, Wk, Wv, Wg, Wo, ln_w, ln_b):
        import jax, jax.numpy as jnp
        import numpy as np
        N_EMBD = 128
        N_HEAD = 16
        N_LAYER = 24
        LAYER_ID = 12
        B, T = (4, 512)
        Q = 64
        EPS = 1e-05 * 64

        def _static_params():
            C, H = (N_EMBD, N_HEAD)
            r01 = LAYER_ID / (N_LAYER - 1)
            r1a0 = 1.0 - LAYER_ID / N_LAYER
            ddd = np.arange(C, dtype=np.float64) / C
            maa_k = (1.0 - ddd ** r1a0).astype(np.float32).reshape(1, 1, C)
            maa_v = (1.0 - (ddd ** r1a0 + 0.3 * r01)).astype(np.float32).reshape(1, 1, C)
            maa_r = (1.0 - ddd ** (0.5 * r1a0)).astype(np.float32).reshape(1, 1, C)
            maa_g = maa_r.copy()
            h = np.arange(H, dtype=np.float64)
            decay = (-6.0 + 5.0 * (h / (H - 1)) ** (0.7 + 1.3 * r01)).astype(np.float32).reshape(H, 1)
            faaaa = (r01 * (1.0 - h / (H - 1))).astype(np.float32).reshape(H, 1)
            return (maa_k, maa_v, maa_r, maa_g, decay, faaaa)

        def _rwkv_forward(x, time_maa_k, time_maa_v, time_maa_r, time_maa_g, time_decay, time_faaaa, Wr, Wk, Wv, Wg, Wo, ln_w, ln_b):
            Bv, Tv, C = x.shape
            H = N_HEAD
            N = C // H
            nC = Tv // Q
            xx = jnp.pad(x, ((0, 0), (1, 0), (0, 0)))[:, :Tv] - x
            xk = x + xx * time_maa_k
            xv = x + xx * time_maa_v
            xr = x + xx * time_maa_r
            xg = x + xx * time_maa_g
            r = (xr @ Wr.T).reshape(Bv, Tv, H, N).transpose(0, 2, 1, 3)
            k = (xk @ Wk.T).reshape(Bv, Tv, H, N).transpose(0, 2, 3, 1)
            v = (xv @ Wv.T).reshape(Bv, Tv, H, N).transpose(0, 2, 1, 3)
            g = jax.nn.gelu(xg @ Wg.T, approximate=False)
            w = jnp.exp(-jnp.exp(time_decay))[:, 0]
            u = time_faaaa[:, 0]
            q = jnp.arange(Q)
            ws = (w ** Q).reshape(1, H, 1, 1)
            wk = (w[:, None] ** (Q - 1 - q)).reshape(1, H, 1, Q)
            wb = (w[:, None] ** q).reshape(1, H, Q, 1)
            i_idx = q[:, None]
            j_idx = q[None, :]
            e = jnp.maximum(i_idx - j_idx - 1, 0)
            Wmat = jnp.where(i_idx > j_idx, w[:, None, None] ** e, 0.0)
            Wmat = Wmat + jnp.eye(Q, dtype=x.dtype) * u[:, None, None]
            Wmat = Wmat.reshape(1, H, Q, Q)
            rr = r.reshape(Bv, H, nC, Q, N).transpose(2, 0, 1, 3, 4)
            kk = k.reshape(Bv, H, N, nC, Q).transpose(3, 0, 1, 2, 4)
            vv = v.reshape(Bv, H, nC, Q, N).transpose(2, 0, 1, 3, 4)

            def step(state, inp):
                rc, kc, vc = inp
                att = rc @ kc
                yc = att * Wmat @ vc + rc @ state * wb
                new_state = ws * state + kc * wk @ vc
                return (new_state, yc)
            state0 = jnp.zeros((Bv, H, N, N), dtype=x.dtype)
            _, ys = jax.lax.scan(step, state0, (rr, kk, vv))
            y = ys.transpose(1, 2, 0, 3, 4).reshape(Bv, H, Tv, N)
            y = y.transpose(0, 2, 1, 3)
            mean = y.mean(axis=-1, keepdims=True)
            var = y.var(axis=-1, keepdims=True)
            yn = (y - mean) / jnp.sqrt(var + EPS)
            yn = yn * ln_w.reshape(1, 1, H, N) + ln_b.reshape(1, 1, H, N)
            yn = yn.reshape(Bv, Tv, C)
            out = yn * g @ Wo.T
            return out
        return _rwkv_forward(x, time_maa_k, time_maa_v, time_maa_r, time_maa_g, time_decay, time_faaaa, Wr, Wk, Wv, Wg, Wo, ln_w, ln_b)

    def _L3_xattn_ref(Q, K, V, wq, wk, wv, wo, bo, w1, b1, w2, b2, ln1_g, ln1_b, ln2_g, ln2_b):
        import jax, jax.numpy as jnp
        import numpy as np
        DIM = 128
        HEADS = 16
        DIM_HEAD = 64
        INNER = HEADS * DIM_HEAD
        MLP = 512
        EPS = 1e-05

        def _layernorm(x, g, b):
            mu = jnp.mean(x, axis=-1, keepdims=True)
            var = jnp.mean(jnp.square(x - mu), axis=-1, keepdims=True)
            return (x - mu) * jax.lax.rsqrt(var + EPS) * g + b

        def _l2norm(x):
            n = jnp.sqrt(jnp.sum(jnp.square(x), axis=-1, keepdims=True))
            return x / jnp.maximum(n, 1e-12)

        def _split_heads(x, B, N):
            return x.reshape(B, N, HEADS, DIM_HEAD).transpose(0, 2, 1, 3)
        B, Nq, _ = Q.shape
        Nk = K.shape[1]
        Qn = _layernorm(Q, ln1_g, ln1_b)
        Kn = _layernorm(K, ln1_g, ln1_b)
        Vn = _layernorm(V, ln1_g, ln1_b)
        q = _split_heads(Qn @ wq, B, Nq)
        k = _split_heads(Kn @ wk, B, Nk)
        v = _split_heads(Vn @ wv, B, Nk)
        qn = _l2norm(q)
        kn = _l2norm(k)
        attn = jnp.einsum('bhqd,bhkd->bhqk', qn, kn)
        out = jnp.einsum('bhqk,bhkd->bhqd', attn, v)
        out = out.transpose(0, 2, 1, 3).reshape(B, Nq, INNER)
        x = Q + out @ wo + bo
        xn = _layernorm(x, ln2_g, ln2_b)
        h = jax.nn.gelu(xn @ w1 + b1, approximate=False)
        return x + h @ w2 + b2

    def _L3_ffn_ref(x, gate_w, gate_b, w1, b1, w2, b2, ln_g, ln_b):
        import jax, jax.numpy as jnp
        import numpy as np
        TOP_K = 2
        TEMP = 0.9
        EPS = 1e-05
        B, S, D, F, E = (2, 256, 128, 512, 8)

        def _moe_forward(x, gate_w, gate_b, w1, b1, w2, b2, ln_g, ln_b):
            logits = (x @ gate_w + gate_b) / TEMP
            topk_vals, topk_idx = jax.lax.top_k(logits, TOP_K)
            keep = jax.nn.one_hot(topk_idx, E, dtype=jnp.bool_).any(-2)
            masked = jnp.where(keep, logits, -jnp.inf)
            gate_probs = jax.nn.softmax(masked, axis=-1)
            h = jnp.einsum('bsd,edf->bsef', x, w1) + b1
            h = jax.nn.gelu(h, approximate=False)
            expert_out = jnp.einsum('bsef,efd->bsed', h, w2) + b2
            out = jnp.einsum('bse,bsed->bsd', gate_probs, expert_out)
            mu = out.mean(-1, keepdims=True)
            var = out.var(-1, keepdims=True)
            out = (out - mu) / jnp.sqrt(var + EPS) * ln_g + ln_b
            return out
        return _moe_forward(x, gate_w, gate_b, w1, b1, w2, b2, ln_g, ln_b)
    x = x + _L0_attn_ref(_layernorm(x, axis=-1), L0_attn_w_qkv, L0_attn_w_proj, L0_attn_b_proj)
    x = x + _L0_xattn_ref(_layernorm(x, axis=-1), ctx_1024, ctx_1024, L0_xattn_Wq, L0_xattn_bq, L0_xattn_Wk, L0_xattn_bk, L0_xattn_Wv, L0_xattn_bv, L0_xattn_Wo, L0_xattn_bo)
    x = x + _L0_ffn_ref(_layernorm(x, axis=-1), L0_ffn_W1, L0_ffn_b1, L0_ffn_W2, L0_ffn_b2, L0_ffn_Wa, L0_ffn_Wb)
    x = x + _L1_attn_ref(_layernorm(x, axis=-1), L1_attn_WQ, L1_attn_bQ, L1_attn_WK, L1_attn_bK, L1_attn_WV, L1_attn_bV, L1_attn_WO, L1_attn_bO, L1_attn_Wg, L1_attn_bg, L1_attn_alpha_logit, L1_attn_ln_gamma, L1_attn_ln_beta)
    x = x + _L1_xattn_ref(_layernorm(x, axis=-1), ctx_1024, ctx_1024, mask_BxS2_ff1, L1_xattn_W_o)
    x = x + _L1_ffn_ref(_layernorm(x, axis=-1), L1_ffn_gate_w, L1_ffn_sh_gate, L1_ffn_sh_up, L1_ffn_sh_down, L1_ffn_rt_gate, L1_ffn_rt_up, L1_ffn_rt_down)
    x = x + _L2_attn_ref(_layernorm(x, axis=-1), L2_attn_w_in, L2_attn_b_in, L2_attn_w_conv, L2_attn_b_conv, L2_attn_w_x, L2_attn_w_dt, L2_attn_A_log, L2_attn_D, L2_attn_w_out)
    x = x + _L2_xattn_ref(_layernorm(x, axis=-1), ctx_1024, L2_xattn_Wq_c, L2_xattn_bq_c, L2_xattn_Wk_s, L2_xattn_bk_s, L2_xattn_Wv_s, L2_xattn_bv_s, L2_xattn_Wq_s, L2_xattn_bq_s, L2_xattn_Wk_c, L2_xattn_bk_c, L2_xattn_Wv_c, L2_xattn_bv_c, L2_xattn_Wg, L2_xattn_bg)
    x = x + _L2_ffn_ref(_layernorm(x, axis=-1), L2_ffn_weight, L2_ffn_ln_gamma, L2_ffn_ln_beta)
    x = x + _L3_attn_ref(_layernorm(x, axis=-1), L3_attn_time_maa_k, L3_attn_time_maa_v, L3_attn_time_maa_r, L3_attn_time_maa_g, L3_attn_time_decay, L3_attn_time_faaaa, L3_attn_Wr, L3_attn_Wk, L3_attn_Wv, L3_attn_Wg, L3_attn_Wo, L3_attn_ln_w, L3_attn_ln_b)
    x = x + _L3_xattn_ref(_layernorm(x, axis=-1), ctx_1024, ctx_1024, L3_xattn_wq, L3_xattn_wk, L3_xattn_wv, L3_xattn_wo, L3_xattn_bo, L3_xattn_w1, L3_xattn_b1, L3_xattn_w2, L3_xattn_b2, L3_xattn_ln1_g, L3_xattn_ln1_b, L3_xattn_ln2_g, L3_xattn_ln2_b)
    x = x + _L3_ffn_ref(_layernorm(x, axis=-1), L3_ffn_gate_w, L3_ffn_gate_b, L3_ffn_w1, L3_ffn_b1, L3_ffn_w2, L3_ffn_b2, L3_ffn_ln_g, L3_ffn_ln_b)
    return x

_drawn_inputs = setup_inputs


def setup_inputs(seed=0):
    import zlib

    import numpy as np

    out = dict(_drawn_inputs(seed))
    spreads = {'L0_xattn_bq': (0.0, 0.1),
     'L0_xattn_bk': (0.0, 0.307),
     'L0_xattn_bv': (0.0, 0.1),
     'L0_xattn_bo': (0.0, 0.1),
     'L0_ffn_b1': (0.0, 0.1),
     'L0_ffn_b2': (0.0, 0.1),
     'L1_attn_ln_gamma': (1.0, 0.2),
     'L1_attn_ln_beta': (0.0, 0.1),
     'L2_attn_D': (1.0, 0.2),
     'L2_ffn_ln_gamma': (1.0, 0.6),
     'L2_ffn_ln_beta': (0.0, 0.739),
     'L3_attn_ln_w': (1.0, 0.6),
     'L3_attn_ln_b': (0.0, 0.8),
     'L3_xattn_bo': (0.0, 0.267),
     'L3_xattn_b1': (0.0, 0.608),
     'L3_xattn_b2': (0.0, 0.268),
     'L3_xattn_ln1_g': (1.0, 0.2),
     'L3_xattn_ln1_b': (0.0, 0.273),
     'L3_xattn_ln2_g': (1.0, 0.6),
     'L3_xattn_ln2_b': (0.0, 0.8),
     'L3_ffn_gate_b': (0.0, 0.1),
     'L3_ffn_b1': (0.0, 0.331),
     'L3_ffn_b2': (0.0, 0.279),
     'L3_ffn_ln_g': (1.0, 0.2),
     'L3_ffn_ln_b': (0.0, 0.381)}
    factors = {'L1_attn_bO': 2.807,
     'L1_attn_alpha_logit': 3.778,
     'L2_attn_b_in': 4.483,
     'L2_attn_b_conv': 5.931,
     'L2_xattn_Wq_c': 8.0,
     'L2_xattn_bq_c': 48.537,
     'L2_xattn_Wk_s': 8.0,
     'L2_xattn_bk_s': 64.0,
     'L2_xattn_bv_s': 6.772,
     'L2_xattn_Wq_s': 8.0,
     'L2_xattn_bq_s': 50.912,
     'L2_xattn_Wk_c': 8.0,
     'L2_xattn_bk_c': 64.0,
     'L2_xattn_bv_c': 8.0,
     'L2_xattn_Wg': 8.0,
     'L2_xattn_bg': 43.979,
     'L3_attn_time_maa_k': 7.371,
     'L3_attn_time_maa_v': 8.0,
     'L3_attn_time_maa_r': 7.468,
     'L3_attn_time_maa_g': 8.0,
     'L3_attn_time_decay': 59.744,
     'L3_attn_time_faaaa': 8.0,
     'L3_attn_Wr': 3.821,
     'L3_attn_Wk': 3.766,
     'L3_attn_Wv': 3.724,
     'L3_attn_Wg': 3.723,
     'L3_attn_Wo': 4.177,
     'L3_xattn_w1': 2.762}
    for name, (base, spread) in spreads.items():
        noise = np.random.default_rng([zlib.crc32(name.encode()), seed]).standard_normal(out[name].shape)
        drawn = base * np.exp(spread * noise) if base else spread * noise
        out[name] = jnp.asarray(drawn.astype(out[name].dtype))
    for name, factor in factors.items():
        out[name] = (out[name] * factor).astype(out[name].dtype)
    return out
```

```python
from contextlib import ExitStack, contextmanager

import concourse.bass as bass
from concourse import mybir

F32 = mybir.dt.float32
I32 = mybir.dt.int32
ALU = mybir.AluOpType
ACT = mybir.ActivationFunctionType
AX = mybir.AxisListType

P = 128
S = 64
D = 128
NT = 4
GT = NT * P
NB = GT // S
H = 16
HH = 8
HD = D // H
VW = 2 * HD + 2
BF16 = mybir.dt.bfloat16
STAGES = tuple(range(1, 13))
LATE = {"L3_ffn": "L0_ffn", "L3_xattn": "L1_attn"}


def semaphores(nc, title, names):
    return {n: nc.alloc_semaphore(f"{title}_{n}") for n in names.split()}


@contextmanager
def block_of(nc, title, names):
    s = semaphores(nc, title, names)
    with nc.Block() as block:
        yield block, s
    nc.clear_and_free_semaphores(list(s.values()))
    nc.all_engine_barrier()


class Chain:

    def __init__(self, eng, sem):
        self.eng, self.sem, self.n = eng, sem, 0

    def step(self, ins):
        self.n += 1
        ins.then_inc(self.sem, 1)
        self.eng.wait_ge(self.sem, self.n)


class Buffers:
    pass


def tiles(t, n=NT):
    return t.rearrange("p (n k) -> p n k", n=n)


def halves(t):
    return t.rearrange("p (b n t) -> p b n t", b=2, t=S)[:, :, 0:4, :]


def spread(t, n):
    return t.unsqueeze(2).broadcast_to([t.shape[0], t.shape[1], n])


def repeat(t, n):
    return t.unsqueeze(1).broadcast_to([t.shape[0], n, t.shape[1]])


LN_SEMS = "ln_stats ln_mean ln_std ln_rstd ln_xn ln_tr ln_xT "
LN2_SEMS = "ln2_stats ln2_mean ln2_std ln2_rstd ln2_xn ln2_tr ln2_xT "


class LayerNorm:

    def __init__(self, e, s, src, dst, eps, dstT=None, bank=None, gain=None, shift=None, pre="ln"):
        self.e, self.src, self.dst, self.eps, self.dstT, self.bank = e, src, dst, eps, dstT, bank
        self.gain, self.shift = gain, shift
        self.stats, self.mean, self.std, self.rstd, self.xn, self.tr, self.xT = (
            s[f"{pre}_{n}"] for n in ("stats", "mean", "std", "rstd", "xn", "tr", "xT"))

    def vector(self, v):
        e = self.e
        for j in range(NT):
            ins = v.bn_stats(e.st[:, 6 * j:6 * j + 6], self.src[:, j * D:(j + 1) * D])
        ins.then_inc(self.stats, 1)
        v.wait_ge(self.stats, 1)
        for j in range(NT):
            ins = v.bn_aggr(e.mv[:, 2 * j:2 * j + 2], e.st[:, 6 * j:6 * j + 6])
        ins.then_inc(self.mean, 1)
        v.wait_ge(self.std, 1)
        v.reciprocal(e.rs[:, 0:NT], e.sd[:, 0:NT]).then_inc(self.rstd, 1)
        v.wait_ge(self.rstd, 1)
        for j in range(NT):
            v.tensor_scalar(self.dst[:, j * D:(j + 1) * D], self.src[:, j * D:(j + 1) * D],
                            e.mv[:, 2 * j:2 * j + 1], e.rs[:, j:j + 1], ALU.subtract, ALU.mult).then_inc(self.xn, 1)

    def scalar(self, a):
        e = self.e
        a.wait_ge(self.mean, 1)
        a.activation(e.sd[:, 0:NT], tiles(e.mv[:, 0:2 * NT])[:, :, 1], ACT.Sqrt,
                     bias=self.eps).then_inc(self.std, 1)
        if self.dstT is not None:
            a.wait_ge(self.tr, 1)
            if self.gain is None:
                a.activation(self.dstT, self.bank_view(), ACT.Copy).then_inc(self.xT, 1)
            else:
                a.activation(self.dstT, self.bank_view(), ACT.Identity, bias=self.shift,
                             scale=self.gain).then_inc(self.xT, 1)

    def bank_view(self):
        if len(self.dstT.shape) == 3:
            return tiles(self.bank, NB)
        return self.bank

    def tensor(self, pe):
        if self.dstT is None:
            return
        for j in range(NT):
            pe.wait_ge(self.xn, j + 1)
            ins = pe.transpose(self.bank[:, j * P:(j + 1) * P], self.dst[:, j * D:(j + 1) * D], self.e.ident)
        ins.then_inc(self.tr, 1)


def transpose_group(pe, e, bank, src):
    for j in range(NT):
        ins = pe.transpose(bank[:, j * P:(j + 1) * P], src[:, j * P:(j + 1) * P], e.ident)
    return ins


def project_out(pe, e, bank, chunks, bias):
    for j in range(NT):
        out = bank[:, j * P:(j + 1) * P]
        for i, (src, w) in enumerate(chunks):
            ins = pe.matmul(out, src[:, j * P:(j + 1) * P], w, start=(i == 0),
                            stop=(bias is None and i == len(chunks) - 1))
        if bias is not None:
            ins = pe.matmul(out, e.ones[0:1, 0:P], bias, start=False, stop=True)
    return ins


def softmax_attention(nc, title, e, q, k, v_src, v_w, v_bias, out_w, out_bias, causal=False, project=None,
                      rope=None, key_mask=False):
    scale = float(HD) ** -0.5
    names = LN_SEMS + ("proj_mm rope_done proj_cp kbd0_done kbd_done v_mm v_ready s_mm s_sub p_ready t_mm pt_cp "
                       "o_mm o_done ot_mm ot_cp y_mm dve_own x_done")
    with block_of(nc, title, names) as (block, s):
        ln = LayerNorm(e, s, e.xt, e.xn, e.eps5, dstT=e.xnT, bank=e.bank(7))
        sbank = lambda j: tiles(e.bank(2 + 2 * (j % 2), 2), 2)
        obank = lambda j: e.bank(6 + j % 2)[:, 0:8 * 2 * VW].rearrange("p (n b c) -> p n b c", n=8, b=2)
        sc = lambda j: e.w0[:, (j % 2) * 1024:(j % 2) * 1024 + 1024]
        pts = lambda j: e.w1[:, (j % 2) * 1024:(j % 2) * 1024 + 1024]
        kbd = lambda j: tiles((e.w3, e.w4)[j % 2], H)
        vbd = e.w2[:, 0:NB * 8 * VW].rearrange("p (b n c) -> p b n c", b=NB, n=8)
        ot = e.w5[:, 0:GT]
        oT = e.w5[:, GT:2 * GT]
        mx, rinv = e.sm[:, 0:16], e.sm[:, 16:32]

        def wait_qk(eng):
            if rope:
                eng.wait_ge(s["rope_done"], 2)
            elif project:
                eng.wait_ge(s["proj_cp"], 2)
            else:
                eng.wait_ge(s["ln_xT"], 1)

        @block.tensor
        def _(pe):
            ln.tensor(pe)
            pe.wait_ge(s["ln_xT"], 1)
            for i, (w, src) in enumerate(rope["mm"] if rope else project or []):
                pe.matmul(e.bank(i), w, src, start=True, stop=True).then_inc(s["proj_mm"], 1)
            wait_qk(pe)
            for b in range(NB):
                out = e.bank(0, 2)[:, b * D:(b + 1) * D]
                for r in range(2):
                    o2 = out[r * S:(r + 1) * S, :]
                    ins = pe.matmul(o2, v_src[:, b * S:(b + 1) * S], v_w, start=True, stop=v_bias is None)
                    if v_bias is not None:
                        ins = pe.matmul(o2, e.ones[0:1, 0:S], v_bias, start=False, stop=True)
            ins.then_inc(s["v_mm"], 1)

            def scores(j):
                if j == 0:
                    pe.wait_ge(s["kbd0_done"], 1)
                else:
                    pe.wait_ge(s["kbd_done"], j)
                if j >= 2:
                    pe.wait_ge(s["s_sub"], j - 1)
                for b2 in range(2):
                    t = (2 * j + b2) * S
                    for i in range(2):
                        out = tiles(sbank(j)[b2 * S:(b2 + 1) * S, i], HH)
                        ins = pe.matmul(out, q[:, t:t + S], kbd(j)[:, i * HH:(i + 1) * HH, b2 * S:(b2 + 1) * S], start=True,
                                        stop=not causal)
                        if causal:
                            ins = pe.matmul(out, e.half[0:S, 0:S], repeat(e.half[0:S, S:2 * S], HH), start=False,
                                            stop=True)
                ins.then_inc(s["s_mm"], 1)

            scores(0)
            scores(1)
            for j in range(NT):
                pe.wait_ge(s["p_ready"], j + 1)
                if j == 0:
                    pe.wait_ge(s["v_ready"], 1)
                else:
                    pe.wait_ge(s["pt_cp"], j)
                for hp in range(H // 2):
                    ins = pe.transpose(e.bank(0, 2)[:, hp * P:(hp + 1) * P], sc(j)[:, hp * P:(hp + 1) * P], e.ident)
                ins.then_inc(s["t_mm"], 1)
                if j + 2 < NT:
                    scores(j + 2)
                pe.wait_ge(s["pt_cp"], j + 1)
                if j >= 2:
                    pe.wait_ge(s["o_done"], j - 1)
                for hp in range(H // 2):
                    ins = pe.matmul(obank(j)[:, hp], pts(j)[:, hp * P:(hp + 1) * P], vbd[:, 2 * j:2 * j + 2, hp],
                                    start=True, stop=True)
                ins.then_inc(s["o_mm"], 1)
            pe.wait_ge(s["o_done"], NT)
            pe.wait_ge(s["s_sub"], NT)
            transpose_group(pe, e, e.bank(2), ot).then_inc(s["ot_mm"], 1)
            pe.wait_ge(s["ot_cp"], 1)
            project_out(pe, e, e.bank(3), [(oT, out_w)], out_bias).then_inc(s["y_mm"], 1)

        @block.gpsimd
        def _(g):
            wait_qk(g)
            for j in range(1, NT):
                if j >= 2:
                    g.wait_ge(s["s_mm"], j - 1)
                g.tensor_tensor(kbd(j), repeat(k[:, j * P:(j + 1) * P], H), spread(e.hmask, P),
                                ALU.mult).then_inc(s["kbd_done"], 1)

        @block.scalar
        def _(a):
            ln.scalar(a)
            if project:
                for i, dst in enumerate((q, k)):
                    a.wait_ge(s["proj_mm"], i + 1)
                    a.activation(dst, e.bank(i), ACT.Copy).then_inc(s["proj_cp"], 1)

            def exps(j):
                a.wait_ge(s["s_sub"], j + 1)
                a.activation(sc(j), sc(j), ACT.Exp, scale=scale).then_inc(s["p_ready"], 1)

            exps(0)
            exps(1)
            for j in range(NT):
                a.wait_ge(s["t_mm"], j + 1)
                if j >= 2:
                    a.wait_ge(s["o_mm"], j - 1)
                a.activation(pts(j), e.bank(0, 2), ACT.Copy).then_inc(s["pt_cp"], 1)
                if j + 2 < NT:
                    exps(j + 2)
            a.wait_ge(s["ot_mm"], 1)
            a.activation(oT, e.bank(2), ACT.Copy).then_inc(s["ot_cp"], 1)

        @block.vector
        def _(v):
            own = Chain(v, s["dve_own"])
            ln.vector(v)
            if rope:
                for i in range(2):
                    b0, b1 = rope["bias"][i]
                    v.wait_ge(s["proj_mm"], 2 * i + 2)
                    v.scalar_tensor_tensor(out=tiles(e.w6[:, 0:GT], NB), in0=tiles(e.bank(2 * i), NB), scalar=b0,
                                           in1=repeat(e.cos, NB), op0=ALU.add, op1=ALU.mult)
                    own.step(v.scalar_tensor_tensor(out=tiles(e.w6[:, GT:2 * GT], NB), in0=tiles(e.bank(2 * i + 1), NB),
                                                    scalar=b1, in1=repeat(e.sin, NB), op0=ALU.add, op1=ALU.mult))
                    v.tensor_tensor((q, k)[i], e.w6[:, 0:GT], e.w6[:, GT:2 * GT], ALU.add).then_inc(s["rope_done"], 1)
                    v.wait_ge(s["rope_done"], i + 1)
            wait_qk(v)
            v.tensor_tensor(kbd(0), repeat(k[:, 0:P], H), spread(e.hmask, P), ALU.mult).then_inc(s["kbd0_done"], 1)
            v.tensor_copy(e.w2[:, 0:NB * 8 * VW].rearrange("p (m c) -> p m c", c=VW)[:, :, 16:VW],
                          repeat(e.headcol, NB * 8))
            v.wait_ge(s["v_mm"], 1)
            v.tensor_tensor(e.w2[:, 0:NB * 8 * VW].rearrange("p (m c) -> p m c", c=VW)[:, :, 0:16],
                            tiles(e.bank(0, 2), NB * 8), repeat(e.vmask, NB * 8), ALU.mult).then_inc(s["v_ready"], 1)

            def front(j):
                v.wait_ge(s["s_mm"], j + 1)
                if j >= 2:
                    v.wait_ge(s["t_mm"], j - 1)
                four = lambda m: m.rearrange("p (g h) k -> p g h k", g=2)
                s3, c3 = sbank(j).rearrange("p g (h k) -> p g h k", h=HH), four(tiles(sc(j), H))
                src = s3
                if key_mask:
                    own.step(v.tensor_tensor(c3, s3, four(repeat(e.kmask[:, j * S:(j + 1) * S], H)), ALU.add))
                    src = c3
                own.step(v.tensor_reduce(tiles(mx, 2), src, AX.X, ALU.max))
                v.tensor_tensor(c3, src, four(spread(mx, S)), ALU.subtract).then_inc(s["s_sub"], 1)
                v.wait_ge(s["s_sub"], j + 1)

            def back(j):
                v.wait_ge(s["o_mm"], j + 1)
                for b2 in range(2):
                    rows = slice(b2 * S, (b2 + 1) * S)
                    ins = v.reciprocal(rinv[rows, :].rearrange("p (n c) -> p n c", c=2), obank(j)[rows, :, b2, 16:VW])
                own.step(ins)
                for b2 in range(2):
                    rows = slice(b2 * S, (b2 + 1) * S)
                    o4 = ot[rows, j * D:(j + 1) * D].rearrange("p (n h d) -> p n h d", n=8, h=2)
                    r4 = rinv[rows, :].rearrange("p (n c) -> p n c", c=2).unsqueeze(3).broadcast_to([S, 8, 2, HD])
                    ins = v.tensor_tensor(o4, obank(j)[rows, :, b2, 0:16].rearrange("p n (h d) -> p n h d", h=2), r4,
                                          ALU.mult)
                ins.then_inc(s["o_done"], 1)
                v.wait_ge(s["o_done"], j + 1)

            front(0)
            front(1)
            for j in range(NT):
                if j + 2 < NT:
                    front(j + 2)
                back(j)
            v.wait_ge(s["y_mm"], 1)
            v.tensor_tensor(e.xt, e.bank(3), e.xt, ALU.add).then_inc(s["x_done"], 1)


def top_mask(v, own, e, vals, keep, n, k, parts=P):
    cmp_, eq = e.w6[0:parts, 0:n * 64], e.w6[0:parts, 512:512 + n * 64]
    shape = [parts, n, 8, 8]
    mine = tiles(vals, n).unsqueeze(3).broadcast_to(shape)
    other = tiles(vals, n).unsqueeze(2).broadcast_to(shape)
    four = lambda t: t.rearrange("p (n a b) -> p n a b", n=n, a=8)
    v.tensor_tensor(four(cmp_), other, mine, ALU.is_gt)
    own.step(v.tensor_tensor(four(eq), other, mine, ALU.is_equal))
    own.step(v.tensor_tensor(tiles(eq, n), tiles(eq, n), repeat(e.lower[0:parts, :], n), ALU.mult))
    own.step(v.tensor_tensor(cmp_, cmp_, eq, ALU.add))
    own.step(v.tensor_reduce(keep, tiles(cmp_, n * 8), AX.X, ALU.add))
    own.step(v.tensor_scalar(keep, keep, float(k) - 0.5, None, ALU.is_lt))


E = 8
FC = 4


def gelu_experts_tensor(pe, e, s, xT, up, down, after_up, after_down):
    def up_mm(x):
        for f in range(FC):
            if x >= 1:
                pe.wait_ge(s["act_done"], FC * (x - 1) + f + 1)
            pe.matmul(e.bank(f), up(x, f), xT, start=True, stop=True).then_inc(s["up_mm"], 1)
        if x in after_up:
            after_up[x]()

    up_mm(0)
    for x in range(E):
        if x + 1 < E:
            up_mm(x + 1)
        pe.wait_ge(s["act_done"], FC * (x + 1))
        if x >= 2:
            pe.wait_ge(s["acc_done"], x - 1)
        h = hidden(e, x)
        project_out(pe, e, e.bank(4 + x % 2), [(h[:, f * GT:(f + 1) * GT], down(x, f)) for f in range(FC)],
                    None).then_inc(s["down_mm"], 1)
        if x in after_down:
            after_down[x]()


def hidden(e, x):
    return (e.w3, e.w4)[x % 2]


def gelu_experts_scalar(a, e, s, func, bias, after):
    for x in range(E):
        for f in range(FC):
            a.wait_ge(s["up_mm"], FC * x + f + 1)
            if x >= 2 and f == 0:
                a.wait_ge(s["down_mm"], x - 1)
            a.activation(hidden(e, x)[:, f * GT:(f + 1) * GT], e.bank(f), func, bias=bias(x, f)).then_inc(s["act_done"], 1)
        if x in after:
            after[x]()


def weighted_sum_vector(v, e, s, acc, wt, n, order):
    for i in range(n):
        v.wait_ge(s["down_mm"], i + 1)
        x = order[i]
        for j in range(NT):
            y = e.bank(4 + i % 2)[:, j * D:(j + 1) * D]
            a = acc[:, j * D:(j + 1) * D]
            if x is None:
                ins = v.tensor_tensor(a, y, a, ALU.add)
            else:
                ins = v.scalar_tensor_tensor(out=a, in0=y, scalar=wt[:, j * E + x:j * E + x + 1], in1=a,
                                             op0=ALU.mult, op1=ALU.add)
        ins.then_inc(s["acc_done"], 1)
        v.wait_ge(s["acc_done"], i + 1)


def zone_ffn(nc, e, W):
    names = LN_SEMS + ("pool_done r1_mm r1_act r2_mm lg_done ex_done w_done wt_mm dve_own up_mm act_done down_mm "
                       "acc_done x_done")
    with block_of(nc, "zone_ffn", names) as (block, s):
        ln = LayerNorm(e, s, e.xt, e.xn, e.eps5, dstT=e.xnT, bank=e.bank(7))
        pooled, hr = e.sm[:, 0:NB], e.sm[0:32, 16:16 + NB]
        lg, mx, keep, sm = e.sm[0:NB, 32:40], e.sm[0:NB, 40:41], e.sm[0:NB, 48:56], e.sm[0:NB, 56:57]
        wt = e.sm[:, 64:64 + NT * E]

        @block.tensor
        def _(pe):
            ln.tensor(pe)
            pe.wait_ge(s["ln_xT"], 1)

            def router_hidden():
                pe.wait_ge(s["pool_done"], 1)
                pe.matmul(e.bank(7)[0:32, 0:NB], W("W1"), pooled, start=True, stop=True).then_inc(s["r1_mm"], 1)

            def router_logits():
                pe.wait_ge(s["r1_act"], 1)
                pe.matmul(e.bank(6)[0:NB, 0:E], hr, W("W2"), start=True, stop=False)
                pe.matmul(e.bank(6)[0:NB, 0:E], e.ones[0:1, 0:NB], W("b2"), start=False, stop=True).then_inc(s["r2_mm"], 1)

            def token_weights():
                pe.wait_ge(s["w_done"], 1)
                for j in range(NT):
                    ins = pe.matmul(e.bank(7)[:, j * E:(j + 1) * E], e.bsel[0:NB, j * P:(j + 1) * P], lg,
                                    start=True, stop=True)
                ins.then_inc(s["wt_mm"], 1)

            gelu_experts_tensor(pe, e, s, e.xnT, lambda x, f: W("Wa")[:, (x * FC + f) * P:(x * FC + f + 1) * P],
                                lambda x, f: W("Wb")[:, (x * FC + f) * D:(x * FC + f + 1) * D],
                                {0: router_hidden, 1: router_logits, 2: token_weights}, {})

        @block.scalar
        def _(a):
            ln.scalar(a)

            def router_hidden():
                a.wait_ge(s["r1_mm"], 1)
                a.activation(hr, e.bank(7)[0:32, 0:NB], ACT.Tanh, bias=W("b1"), scale=1.0 / S).then_inc(s["r1_act"], 1)

            def numerators():
                a.wait_ge(s["lg_done"], 1)
                a.activation(lg, lg, ACT.Exp).then_inc(s["ex_done"], 1)

            gelu_experts_scalar(a, e, s, ACT.Gelu_apprx_tanh, lambda x, f: 0.0, {0: router_hidden, 1: numerators})

        @block.vector
        def _(v):
            own = Chain(v, s["dve_own"])
            ln.vector(v)
            v.wait_ge(s["ln_xT"], 1)
            v.tensor_reduce(pooled, tiles(e.xnT, NB), AX.X, ALU.add).then_inc(s["pool_done"], 1)
            v.wait_ge(s["r2_mm"], 1)
            own.step(v.tensor_reduce(mx, e.bank(6)[0:NB, 0:E], AX.X, ALU.max))
            v.tensor_scalar(lg, e.bank(6)[0:NB, 0:E], mx, None, ALU.subtract).then_inc(s["lg_done"], 1)
            v.wait_ge(s["ex_done"], 1)
            top_mask(v, own, e, lg, keep, 1, 3, NB)
            own.step(v.tensor_tensor(lg, lg, keep, ALU.mult))
            own.step(v.tensor_reduce(sm, lg, AX.X, ALU.add))
            own.step(v.reciprocal(sm, sm))
            v.tensor_scalar(lg, lg, sm, None, ALU.mult).then_inc(s["w_done"], 1)
            v.wait_ge(s["wt_mm"], 1)
            own.step(v.tensor_copy(wt, e.bank(7)[:, 0:NT * E]))
            own.step(v.tensor_tensor(e.xt, e.xt, e.xn, ALU.add))
            weighted_sum_vector(v, e, s, e.xt, wt, E, list(range(E)))


def top1_ffn(nc, e, W):
    IC = 2
    n = E + 1
    names = LN_SEMS + "lg_mm mx_done score_done xs_done xs_mm xs_cp dve_own gu_mm silu_done act_done down_mm acc_done x_done"
    with block_of(nc, "top1_ffn", names) as (block, s):
        ln = LayerNorm(e, s, e.xt, e.xn, e.eps5, dstT=e.xnT, bank=e.bank(7))
        lg, mx, keep = e.sm[:, 0:32], e.sm[:, 32:36], e.sm[:, 40:72]
        score = e.sm[:, 36:40]
        xs, xsT = e.w5[:, 0:GT], e.w5[:, GT:2 * GT]
        order = [None] + list(range(E))
        sil = lambda i: e.w1[:, (i % 2) * 1024:(i % 2) * 1024 + 1024]
        act = lambda i: e.w2[:, (i % 2) * 1024:(i % 2) * 1024 + 1024]

        @block.tensor
        def _(pe):
            ln.tensor(pe)
            pe.wait_ge(s["ln_xT"], 1)
            project = lambda j: pe.matmul(e.bank(6)[:, j * E:(j + 1) * E], e.xnT[:, j * P:(j + 1) * P], W("gate_w"),
                                          start=True, stop=True)
            for j in range(NT):
                ins = project(j)
            ins.then_inc(s["lg_mm"], 1)

            def gate_up(i):
                x = order[i]
                if i >= 1:
                    pe.wait_ge(s["silu_done"], IC * i)
                    pe.wait_ge(s["act_done"], IC * i)
                if i == 1:
                    pe.wait_ge(s["xs_done"], NT)
                    transpose_group(pe, e, e.bank(7), xs).then_inc(s["xs_mm"], 1)
                    pe.wait_ge(s["xs_cp"], 1)
                src = e.xnT if x is None else xsT
                for c in range(IC):
                    for k, w in enumerate(("gate", "up")):
                        wt = W("sh_" + w)[:, c * P:(c + 1) * P] if x is None else \
                            W("rt_" + w)[:, (x * IC + c) * P:(x * IC + c + 1) * P]
                        pe.matmul(e.bank(2 * k + c), wt, src, start=True, stop=True).then_inc(s["gu_mm"], 1)

            gate_up(0)
            for i in range(n):
                if i + 1 < n:
                    gate_up(i + 1)
                x = order[i]
                pe.wait_ge(s["act_done"], IC * (i + 1))
                if i >= 2:
                    pe.wait_ge(s["acc_done"], i - 1)
                dw = lambda c: W("sh_down")[:, c * D:(c + 1) * D] if x is None else \
                    W("rt_down")[:, (x * IC + c) * D:(x * IC + c + 1) * D]
                project_out(pe, e, e.bank(4 + i % 2), [(act(i)[:, c * GT:(c + 1) * GT], dw(c)) for c in range(IC)],
                            None).then_inc(s["down_mm"], 1)

        @block.scalar
        def _(a):
            ln.scalar(a)
            a.wait_ge(s["mx_done"], 1)
            a.activation(score, mx, ACT.Sigmoid).then_inc(s["score_done"], 1)
            for i in range(n):
                if i == 1:
                    a.wait_ge(s["xs_mm"], 1)
                    a.activation(xsT, e.bank(7), ACT.Copy).then_inc(s["xs_cp"], 1)
                for c in range(IC):
                    a.wait_ge(s["gu_mm"], 2 * IC * i + 2 * c + 1)
                    if i >= 2:
                        a.wait_ge(s["act_done"], IC * (i - 1))
                    a.activation(sil(i)[:, c * GT:(c + 1) * GT], e.bank(c), ACT.Silu).then_inc(s["silu_done"], 1)

        @block.vector
        def _(v):
            own = Chain(v, s["dve_own"])
            ln.vector(v)
            v.wait_ge(s["lg_mm"], 1)
            own.step(v.tensor_copy(lg, e.bank(6)[:, 0:32]))
            own.step(v.tensor_reduce(mx, tiles(lg), AX.X, ALU.max))
            v.engine_nop().then_inc(s["mx_done"], 1)
            top_mask(v, own, e, lg, keep, NT, 1)
            v.wait_ge(s["score_done"], 1)
            for j in range(NT):
                v.tensor_scalar(xs[:, j * D:(j + 1) * D], e.xn[:, j * D:(j + 1) * D], score[:, j:j + 1], None,
                                ALU.mult).then_inc(s["xs_done"], 1)

            def gated(i):
                for c in range(IC):
                    v.wait_ge(s["silu_done"], IC * i + c + 1)
                    v.wait_ge(s["gu_mm"], 2 * IC * i + 2 * c + 2)
                    if i >= 2:
                        v.wait_ge(s["down_mm"], i - 1)
                    v.tensor_tensor(act(i)[:, c * GT:(c + 1) * GT], e.bank(2 + c), sil(i)[:, c * GT:(c + 1) * GT],
                                    ALU.mult).then_inc(s["act_done"], 1)

            gated(0)
            for i in range(n):
                if i + 1 < n:
                    gated(i + 1)
                v.wait_ge(s["down_mm"], i + 1)
                for j in range(NT):
                    y, x = e.bank(4 + i % 2)[:, j * D:(j + 1) * D], e.xt[:, j * D:(j + 1) * D]
                    if order[i] is None:
                        ins = v.tensor_tensor(x, y, x, ALU.add)
                    else:
                        k = j * E + order[i]
                        ins = v.scalar_tensor_tensor(out=x, in0=y, scalar=keep[:, k:k + 1], in1=x, op0=ALU.mult,
                                                     op1=ALU.add)
                ins.then_inc(s["acc_done"], 1)
                v.wait_ge(s["acc_done"], i + 1)


WC = 8


def decay_attention(nc, e, W):
    names = LN_SEMS + LN2_SEMS + ("qkgv_mm q_done k_done g_done v_done at_mm at_done o_mm og_done y_mm "
                                  "dve_own x_done")
    with block_of(nc, "decay_attention", names) as (block, s):
        ln = LayerNorm(e, s, e.xt, e.xn, e.eps5)
        ln2 = LayerNorm(e, s, e.xn, e.w6[:, 0:GT], e.eps5, dstT=e.xnT, bank=e.bank(7), gain=W("ln_gamma"),
                        shift=W("ln_beta"), pre="ln2")
        par = lambda t, c: t[:, (c % 2) * GT:(c % 2 + 1) * GT]
        qd = lambda c: par(e.w0, c)
        k1 = lambda c: par(e.w0[:, 1024:2048], c)
        k2 = lambda c: par(e.w1, c)
        gate = lambda c: par(e.w1[:, 1024:2048], c)
        vs = lambda c: par(e.w2, c)
        at = lambda c: par(e.atz, c)
        og = lambda c: (e.w3 if c < 4 else e.w4)[:, (c % 4) * GT:(c % 4 + 1) * GT]

        @block.tensor
        def _(pe):
            ln2.tensor(pe)
            pe.wait_ge(s["ln2_xT"], 1)

            def project(c):
                col = slice(c * P, (c + 1) * P)
                for i, w in enumerate(("WQ", "WK", "Wg")):
                    if c >= 1:
                        pe.wait_ge((s["q_done"], s["k_done"], s["g_done"])[i], c)
                    pe.matmul(e.bank(i), W(w)[:, col], e.xnT, start=True, stop=True).then_inc(s["qkgv_mm"], 1)
                if c >= 1:
                    pe.wait_ge(s["v_done"], c)
                project_out(pe, e, e.bank(3), [(e.xnT, W("WV")[:, col])], W("bV")[:, col]).then_inc(s["qkgv_mm"], 1)

            project(0)
            for c in range(WC):
                pe.wait_ge(s["q_done"], c + 1)
                pe.wait_ge(s["k_done"], c + 1)
                if c >= 1:
                    pe.wait_ge(s["at_done"], c)
                for b in range(NB):
                    r0 = (b % 2) * S
                    for h in range(2):
                        rows, col = slice(h * S, (h + 1) * S), (b // 2) * S
                        out = e.bank(4 + h)
                        pe.matmul(out[r0:r0 + 32, col:col + 32], k1(c)[rows, b * S:b * S + 32],
                                  qd(c)[rows, b * S:b * S + 32], start=True, stop=True)
                        ins = pe.matmul(out[r0:r0 + S, col + 32:col + S], k2(c)[rows, b * S:(b + 1) * S],
                                        qd(c)[rows, b * S + 32:(b + 1) * S], start=True, stop=True)
                ins.then_inc(s["at_mm"], 1)
                if c + 1 < WC:
                    project(c + 1)
                pe.wait_ge(s["at_done"], c + 1)
                pe.wait_ge(s["v_done"], c + 1)
                if c >= 1:
                    pe.wait_ge(s["og_done"], c)
                for b in range(NB):
                    r0 = slice((b % 2) * S, (b % 2 + 1) * S)
                    for h in range(2):
                        vc, ac = (b // 2) * P + h * S, h * 256 + (b // 2) * S
                        ins = pe.matmul(e.bank(6 + b % 2)[h * S:(h + 1) * S, (b // 2) * S:(b // 2 + 1) * S],
                                        vs(c)[r0, vc:vc + S], at(c)[r0, ac:ac + S], start=True, stop=True)
                ins.then_inc(s["o_mm"], 1)
            pe.wait_ge(s["og_done"], WC)
            project_out(pe, e, e.bank(0), [(og(c), W("WO")[:, c * D:(c + 1) * D]) for c in range(WC)],
                        W("bO")).then_inc(s["y_mm"], 1)

        @block.scalar
        def _(a):
            ln.scalar(a)
            ln2.scalar(a)
            for c in range(WC):
                a.wait_ge(s["qkgv_mm"], 4 * c + 3)
                if c >= 2:
                    a.wait_ge(s["og_done"], c - 1)
                a.activation(gate(c), e.bank(2), ACT.Silu, bias=W("bg")[:, c:c + 1]).then_inc(s["g_done"], 1)
                a.wait_ge(s["qkgv_mm"], 4 * c + 4)
                if c >= 2:
                    a.wait_ge(s["o_mm"], c - 1)
                a.activation(vs(c), e.bank(3), ACT.Copy).then_inc(s["v_done"], 1)

        @block.vector
        def _(v):
            ln.vector(v)
            v.wait_ge(s["ln_xn"], NT)
            ln2.vector(v)

            def scaled(c):
                q8, k8 = tiles(e.bank(0), NB), tiles(e.bank(1), NB)
                v.wait_ge(s["qkgv_mm"], 4 * c + 1)
                if c >= 2:
                    v.wait_ge(s["at_mm"], c - 1)
                v.scalar_tensor_tensor(out=tiles(qd(c), NB), in0=q8, scalar=W("bQ")[:, c:c + 1],
                                       in1=repeat(e.pq[:, c * S:(c + 1) * S], NB), op0=ALU.add,
                                       op1=ALU.mult).then_inc(s["q_done"], 1)
                v.wait_ge(s["qkgv_mm"], 4 * c + 2)
                v.scalar_tensor_tensor(out=tiles(k1(c), NB)[:, :, 0:32], in0=k8[:, :, 0:32], scalar=W("bK")[:, c:c + 1],
                                       in1=repeat(e.pk1[:, c * 32:(c + 1) * 32], NB), op0=ALU.add, op1=ALU.mult)
                v.scalar_tensor_tensor(out=tiles(k2(c), NB), in0=k8, scalar=W("bK")[:, c:c + 1],
                                       in1=repeat(e.pk2[:, c * S:(c + 1) * S], NB), op0=ALU.add,
                                       op1=ALU.mult).then_inc(s["k_done"], 1)

            scaled(0)
            for c in range(WC):
                v.wait_ge(s["at_mm"], c + 1)
                if c >= 2:
                    v.wait_ge(s["o_mm"], c - 1)
                for rows, t in ((slice(0, P), slice(32, S)), (slice(0, 32), slice(0, 32)), (slice(S, S + 32), slice(0, 32))):
                    n = rows.stop - rows.start
                    mask = e.tri[rows, t].unsqueeze(1).unsqueeze(1).broadcast_to([n, 2, 4, 32]).bitcast(I32)
                    ins = v.copy_predicated(at(c).rearrange("p (b n t) -> p b n t", b=2, t=S)[rows, :, :, t], mask,
                                            halves(e.bank(4, 2))[rows, :, :, t])
                ins.then_inc(s["at_done"], 1)
                if c + 1 < WC:
                    scaled(c + 1)
                v.wait_ge(s["o_mm"], c + 1)
                v.wait_ge(s["g_done"], c + 1)
                v.tensor_tensor(og(c).rearrange("p (n b t) -> p b n t", b=2, t=S), halves(e.bank(6, 2)),
                                gate(c).rearrange("p (n b t) -> p b n t", b=2, t=S), ALU.mult).then_inc(s["og_done"], 1)
            own = Chain(v, s["dve_own"])
            own.step(v.tensor_tensor(e.xt, e.xt, e.xn, ALU.add))
            v.wait_ge(s["y_mm"], 1)
            v.tensor_tensor(e.xt, e.bank(0), e.xt, ALU.add).then_inc(s["x_done"], 1)


def norm_attention_mlp(nc, e, W):
    names = LN_SEMS + LN2_SEMS + ("qkv_mm q_cp k_sq v_cp ss_mm ss_rec rn_done krn_rec krn_done qn_done kn_done m_mm m_cp "
                                  "o_mm og_done y_mm dve_own")
    with block_of(nc, "norm_attention_mlp", names) as (block, s):
        ln = LayerNorm(e, s, e.xt, e.xn, e.eps5)
        ln2 = LayerNorm(e, s, e.xn, e.w6[:, 0:GT], e.eps5, dstT=e.xnT, bank=e.bank(7), gain=W("ln1_g"),
                        shift=W("ln1_b"), pre="ln2")
        par = lambda t, c: t[:, (c % 2) * GT:(c % 2 + 1) * GT]
        q = lambda c: e.w0[:, (c % 3) * GT:(c % 3 + 1) * GT]
        q2 = e.w0[:, 3 * GT:4 * GT]
        k2, kn = (lambda c: par(e.w1, c)), (lambda c: par(e.w1[:, 1024:2048], c))
        vs, ms = (lambda c: par(e.w2, c)), (lambda c: par(e.w5, c))
        rn = lambda c: par(e.atz, c)
        kss = lambda c: e.sm[:, (c % 2) * 8:(c % 2) * 8 + 8]
        og = lambda c: (e.w3 if c < 4 else e.w4)[:, (c % 4) * GT:(c % 4 + 1) * GT]

        @block.tensor
        def _(pe):
            ln2.tensor(pe)
            pe.wait_ge(s["ln2_xT"], 1)

            def project(c):
                col = slice(c * P, (c + 1) * P)
                if c >= 1:
                    pe.wait_ge(s["q_cp"], c)
                pe.matmul(e.bank(0), W("wq")[:, col], e.xnT, start=True, stop=True).then_inc(s["qkv_mm"], 1)
                if c >= 1:
                    pe.wait_ge(s["kn_done"], c)
                project_out(pe, e, e.bank(2), [(e.ctxT, W("wk")[:, col])], None).then_inc(s["qkv_mm"], 1)
                if c >= 1:
                    pe.wait_ge(s["v_cp"], c)
                project_out(pe, e, e.bank(3), [(e.ctxT, W("wv")[:, col])], None).then_inc(s["qkv_mm"], 1)
                pe.wait_ge(s["q_cp"], c + 1)
                if c >= 1:
                    pe.wait_ge(s["ss_rec"], c)
                pe.matmul(e.bank(1), e.headblk, q2, start=True, stop=True).then_inc(s["ss_mm"], 1)

            def keys_values(c):
                pe.wait_ge(s["kn_done"], c + 1)
                pe.wait_ge(s["v_cp"], c + 1)
                if c >= 1:
                    pe.wait_ge(s["m_cp"], c)
                for b in range(NB):
                    r0 = slice((b % 2) * S, (b % 2 + 1) * S)
                    for h in range(2):
                        col = slice((b // 2) * P + h * S, (b // 2) * P + (h + 1) * S)
                        ins = pe.matmul(e.bank(4 + b % 2)[h * S:(h + 1) * S, (b // 2) * S:(b // 2 + 1) * S], kn(c)[r0, col],
                                        vs(c)[r0, col], start=True, stop=True)
                ins.then_inc(s["m_mm"], 1)

            def heads(c):
                pe.wait_ge(s["m_cp"], c + 1)
                pe.wait_ge(s["qn_done"], c + 1)
                if c >= 2:
                    pe.wait_ge(s["og_done"], c - 1)
                for b in range(NB):
                    col = slice(b * S, (b + 1) * S)
                    for h in range(2):
                        r0 = slice(h * S, (h + 1) * S)
                        ins = pe.matmul(e.bank(6 + c % 2)[r0, col], ms(c)[r0, col], q(c)[r0, col],
                                        start=True, stop=True)
                ins.then_inc(s["o_mm"], 1)

            project(0)
            for c in range(WC):
                if c + 1 < WC:
                    project(c + 1)
                keys_values(c)
                if c >= 1:
                    heads(c - 1)
            heads(WC - 1)
            pe.wait_ge(s["og_done"], WC)
            project_out(pe, e, e.bank(0), [(og(c), W("wo")[:, c * D:(c + 1) * D]) for c in range(WC)],
                        W("bo")).then_inc(s["y_mm"], 1)

        @block.scalar
        def _(a):
            ln.scalar(a)
            ln2.scalar(a)

            def squares(c):
                a.wait_ge(s["qkv_mm"], 3 * c + 1)
                if c >= 3:
                    a.wait_ge(s["o_mm"], c - 2)
                a.activation(q(c), e.bank(0), ACT.Copy)
                if c >= 1:
                    a.wait_ge(s["ss_mm"], c)
                a.activation(q2, e.bank(0), ACT.Square).then_inc(s["q_cp"], 1)
                a.wait_ge(s["qkv_mm"], 3 * c + 2)
                a.activation(k2(c), e.bank(2), ACT.Square).then_inc(s["k_sq"], 1)
                a.wait_ge(s["qkv_mm"], 3 * c + 3)
                if c >= 2:
                    a.wait_ge(s["m_mm"], c - 1)
                a.activation(vs(c), e.bank(3), ACT.Copy).then_inc(s["v_cp"], 1)
                a.wait_ge(s["krn_rec"], c + 1)
                a.activation(kss(c), kss(c), ACT.Sqrt).then_inc(s["krn_done"], 1)

            def query_factors(c):
                a.wait_ge(s["ss_rec"], c + 1)
                a.activation(rn(c), rn(c), ACT.Sqrt).then_inc(s["rn_done"], 1)

            def copy_heads(c):
                a.wait_ge(s["o_mm"], c + 1)
                a.activation(og(c), e.bank(6 + c % 2), ACT.Copy).then_inc(s["og_done"], 1)

            squares(0)
            query_factors(0)
            for c in range(WC):
                if c + 1 < WC:
                    squares(c + 1)
                a.wait_ge(s["m_mm"], c + 1)
                if c >= 2:
                    a.wait_ge(s["o_mm"], c - 1)
                a.activation(ms(c).rearrange("p (n b t) -> p b n t", b=2, t=S), halves(e.bank(4, 2)), ACT.Copy).then_inc(s["m_cp"], 1)
                if c + 1 < WC:
                    query_factors(c + 1)
                if c >= 1:
                    copy_heads(c - 1)
            copy_heads(WC - 1)

        @block.vector
        def _(v):
            own = Chain(v, s["dve_own"])
            ln.vector(v)
            v.wait_ge(s["ln_xn"], NT)
            ln2.vector(v)
            for c in range(WC):
                v.wait_ge(s["k_sq"], c + 1)
                own.step(v.tensor_reduce(kss(c), tiles(k2(c), 8), AX.X, ALU.add))
                own.step(v.tensor_scalar(kss(c), kss(c), 1e-24, None, ALU.max))
                v.reciprocal(kss(c), kss(c)).then_inc(s["krn_rec"], 1)
                v.wait_ge(s["krn_done"], c + 1)
                if c >= 2:
                    v.wait_ge(s["m_mm"], c - 1)
                v.tensor_tensor(tiles(kn(c), 8), tiles(e.bank(2), 8), spread(kss(c), S), ALU.mult).then_inc(s["kn_done"], 1)
                v.wait_ge(s["ss_mm"], c + 1)
                own.step(v.tensor_scalar(rn(c), e.bank(1), 1e-24, None, ALU.max))
                v.reciprocal(rn(c), rn(c)).then_inc(s["ss_rec"], 1)
                v.wait_ge(s["rn_done"], c + 1)
                v.tensor_tensor(q(c), q(c), rn(c), ALU.mult).then_inc(s["qn_done"], 1)
            v.wait_ge(s["y_mm"], 1)
            own.step(v.tensor_tensor(e.x2, e.bank(0), e.xn, ALU.add))
            own.step(v.tensor_tensor(e.xt, e.x2, e.xt, ALU.add))

    names = LN_SEMS + "up_mm act_done y_mm x_done"
    with block_of(nc, "norm_attention_mlp_2", names) as (block, s):
        ln = LayerNorm(e, s, e.x2, e.xn, e.eps5, dstT=e.xnT, bank=e.bank(7), gain=W("ln2_g"), shift=W("ln2_b"))

        @block.tensor
        def _(pe):
            ln.tensor(pe)
            pe.wait_ge(s["ln_xT"], 1)
            for f in range(FC):
                pe.matmul(e.bank(f), W("w1")[:, f * P:(f + 1) * P], e.xnT, start=True, stop=True).then_inc(s["up_mm"], 1)
            pe.wait_ge(s["act_done"], FC)
            project_out(pe, e, e.bank(4), [(e.w3[:, f * GT:(f + 1) * GT], W("w2")[:, f * D:(f + 1) * D])
                                           for f in range(FC)], W("b2")).then_inc(s["y_mm"], 1)

        @block.scalar
        def _(a):
            ln.scalar(a)
            for f in range(FC):
                a.wait_ge(s["up_mm"], f + 1)
                a.activation(e.w3[:, f * GT:(f + 1) * GT], e.bank(f), ACT.Gelu, bias=W("b1")[:, f:f + 1]
                             ).then_inc(s["act_done"], 1)

        @block.vector
        def _(v):
            ln.vector(v)
            v.wait_ge(s["y_mm"], 1)
            v.tensor_tensor(e.xt, e.bank(4), e.xt, ALU.add).then_inc(s["x_done"], 1)


def state_space(nc, e, W):
    N = 16
    names = LN_SEMS + ("xr_mm xc_cp res_cp conv_done u_done dbc_mm dt_cp hi_cp bc_parts dp_mm sp_done dl_done du_done "
                       "b_mm c_mm a_done b_cp bu_done hs_done hc_done acc_mm yo_done y_mm act_own dve_own x_done")
    with block_of(nc, "state_space", names) as (block, s):
        ln = LayerNorm(e, s, e.xt, e.xn, e.eps5, dstT=e.xnT, bank=e.bank(7))
        two = lambda t, c: t[:, c * GT:(c + 1) * GT]
        xp = lambda c: tiles(e.xpad[:, c * NB * (S + 3):(c + 1) * NB * (S + 3)], NB)
        u = lambda c: two(e.w0, c)
        res = lambda c: two(e.w0, 2 + c)
        delta = lambda c: two(e.w1, c)
        du = lambda c: two(e.w1, 2 + c)
        bs = lambda n: two(e.w2, n % 2)
        bbank, cbank = (lambda n: e.bank((0, 1, 4)[n % 3])), (lambda n: e.bank((2, 3, 5)[n % 3]))
        dts, rest = e.w5[0:64, 0:GT], e.w5[0:32, GT:2 * GT]
        at = lambda c, n: two(e.adec, 2 * (n % 2) + c)
        bu = lambda c, n: two((e.w3, e.w2)[c], 2 * c + n % 2)
        hs = lambda c, n: two(e.w3, 2 + c) if n % 2 else (e.w5[:, 0:GT], e.xn)[c]
        hc = lambda c, n: two(e.w4, 2 * (n % 2) + c)
        tmp = lambda c: two(e.w6, c)

        @block.tensor
        def _(pe):
            ln.tensor(pe)
            pe.wait_ge(s["ln_xT"], 1)
            for m in range(4):
                pe.matmul(e.bank(m), W("w_in")[:, m * P:(m + 1) * P], e.xnT, start=True, stop=True).then_inc(s["xr_mm"], 1)
            pe.wait_ge(s["u_done"], 2)
            for b, (k, lo) in ((4, (64, 0)), (5, (32, 64))):
                for c in range(2):
                    ins = pe.matmul(e.bank(b)[0:k, :], W("w_x")[:, c * 96 + lo:c * 96 + lo + k], u(c),
                                    start=(c == 0), stop=(c == 1))
                ins.then_inc(s["dbc_mm"], 1)
            pe.wait_ge(s["dt_cp"], 1)
            for c in range(2):
                pe.matmul(e.bank(6 + c), W("w_dt")[:, c * P:(c + 1) * P], dts, start=True, stop=True).then_inc(s["dp_mm"], 1)
            pe.wait_ge(s["bc_parts"], 1)
            pe.wait_ge(s["xc_cp"], 2)
            pe.wait_ge(s["res_cp"], 2)

            def row_of(out, row):
                return pe.matmul(out, e.sel[:, row:row + 1].broadcast_to([96, P]), e.bcp, start=True, stop=True)

            def b_row(n):
                if n >= 3:
                    pe.wait_ge(s["b_cp"], n - 2)
                row_of(bbank(n), n).then_inc(s["b_mm"], 1)

            def c_row(n):
                if n >= 3:
                    pe.wait_ge(s["hc_done"], 2 * (n - 2))
                row_of(cbank(n), N + n).then_inc(s["c_mm"], 1)

            for n in range(3):
                b_row(n)
                c_row(n)
            pe.wait_ge(s["dl_done"], 2)
            for n in range(N):
                if n + 3 < N:
                    b_row(n + 3)
                for c in range(2):
                    pe.wait_ge(s["hc_done"], 2 * n + c + 1)
                    pe.matmul(e.bank(6 + c), e.ident, hc(c, n), start=(n == 0), stop=(n == N - 1)).then_inc(s["acc_mm"], 1)
                if n + 3 < N:
                    c_row(n + 3)
            pe.wait_ge(s["yo_done"], 2)
            project_out(pe, e, e.bank(4), [(tmp(c), W("w_out")[:, c * D:(c + 1) * D]) for c in range(2)],
                        None).then_inc(s["y_mm"], 1)

        @block.scalar
        def _(a):
            own = Chain(a, s["act_own"])
            ln.scalar(a)
            for m in range(4):
                a.wait_ge(s["xr_mm"], m + 1)
                if m < 2:
                    a.activation(xp(m)[:, :, 3:3 + S], tiles(e.bank(m), NB), ACT.Identity,
                                 bias=W("b_in")[:, m:m + 1]).then_inc(s["xc_cp"], 1)
                else:
                    a.activation(res(m - 2), e.bank(m), ACT.Silu, bias=W("b_in")[:, m:m + 1]).then_inc(s["res_cp"], 1)
            for c in range(2):
                a.wait_ge(s["conv_done"], c + 1)
                a.activation(u(c), tmp(c), ACT.Silu, bias=W("b_conv")[:, c:c + 1]).then_inc(s["u_done"], 1)
            a.wait_ge(s["dbc_mm"], 1)
            a.activation(dts, e.bank(4)[0:64, :], ACT.Copy).then_inc(s["dt_cp"], 1)
            a.wait_ge(s["dbc_mm"], 2)
            a.activation(e.bcp[0:32, :], e.bank(5)[0:32, :], ACT.Copy).then_inc(s["hi_cp"], 1)
            for c in range(2):
                a.wait_ge(s["dp_mm"], c + 1)
                ins = a.activation(delta(c), e.bank(6 + c), ACT.Abs)
            own.step(ins)
            for c in range(2):
                ins = a.activation(delta(c), delta(c), ACT.Exp, scale=-1.0)
            own.step(ins)
            for c in range(2):
                a.activation(delta(c), delta(c), ACT.Ln, bias=1.0).then_inc(s["sp_done"], 1)
            for n in range(N):
                a.wait_ge(s["b_mm"], n + 1)
                if n >= 2:
                    a.wait_ge(s["bu_done"], 2 * (n - 1))
                a.activation(bs(n), bbank(n), ACT.Copy).then_inc(s["b_cp"], 1)
                for c in range(2):
                    if n == 0:
                        a.wait_ge(s["dl_done"], c + 1)
                    if n >= 2:
                        a.wait_ge(s["hs_done"], 2 * (n - 2) + c + 1)
                    a.activation(tiles(at(c, n), NB)[:, :, 1:S], tiles(delta(c), NB)[:, :, 1:S], ACT.Exp,
                                 scale=e.aneg[:, c * N + n:c * N + n + 1]).then_inc(s["a_done"], 1)

        @block.vector
        def _(v):
            own = Chain(v, s["dve_own"])
            ln.vector(v)
            for c in range(2):
                v.wait_ge(s["xc_cp"], c + 1)
                t = tiles(tmp(c), NB)
                own.step(v.tensor_scalar(t, xp(c)[:, :, 0:S], W("w_conv")[:, c * 4:c * 4 + 1], None, ALU.mult))
                for k in range(1, 4):
                    ins = v.scalar_tensor_tensor(out=t, in0=xp(c)[:, :, k:k + S], scalar=W("w_conv")[:, c * 4 + k:c * 4 + k + 1],
                                                 in1=t, op0=ALU.mult, op1=ALU.add)
                    if k < 3:
                        own.step(ins)
                ins.then_inc(s["conv_done"], 1)
            v.wait_ge(s["hi_cp"], 1)
            raw = e.bank(5)[0:32, :]
            own.step(v.tensor_tensor(rest, raw, e.bcp[0:32, :], ALU.subtract))
            own.step(v.tensor_copy(e.bcp[32:64, :], rest))
            own.step(v.tensor_copy(e.bcm, rest))
            own.step(v.tensor_tensor(rest, rest, e.bcm, ALU.subtract))
            v.tensor_copy(e.bcp[64:96, :], rest).then_inc(s["bc_parts"], 1)
            for c in range(2):
                v.wait_ge(s["sp_done"], c + 1)
                v.scalar_tensor_tensor(out=delta(c), in0=e.bank(6 + c), scalar=0.0, in1=delta(c), op0=ALU.max,
                                       op1=ALU.add).then_inc(s["dl_done"], 1)
            v.wait_ge(s["dl_done"], 2)
            v.wait_ge(s["u_done"], 2)
            for c in range(2):
                v.tensor_tensor(du(c), delta(c), u(c), ALU.mult).then_inc(s["du_done"], 1)

            def contribute(n):
                v.wait_ge(s["hs_done"], 2 * n + 2)
                v.wait_ge(s["c_mm"], n + 1)
                for c in range(2):
                    if n >= 2:
                        v.wait_ge(s["acc_mm"], 2 * (n - 2) + c + 1)
                    v.tensor_tensor(hc(c, n), hs(c, n), cbank(n), ALU.mult).then_inc(s["hc_done"], 1)

            for n in range(N):
                for c in range(2):
                    v.wait_ge(s["bu_done"], 2 * n + c + 1)
                    v.wait_ge(s["a_done"], 2 * n + c + 1)
                    if n >= 2:
                        v.wait_ge(s["hc_done"], 2 * (n - 2) + c + 1)
                    v.tensor_tensor_scan(hs(c, n), at(c, n), bu(c, n), 0.0, ALU.mult, ALU.add).then_inc(s["hs_done"], 1)
                if n >= 1:
                    contribute(n - 1)
            contribute(N - 1)
            v.wait_ge(s["acc_mm"], 2 * N)
            for c in range(2):
                ins = v.scalar_tensor_tensor(out=tmp(c), in0=u(c), scalar=W("D")[:, c:c + 1], in1=e.bank(6 + c),
                                             op0=ALU.mult, op1=ALU.add)
            own.step(ins)
            for c in range(2):
                v.tensor_tensor(tmp(c), tmp(c), res(c), ALU.mult).then_inc(s["yo_done"], 1)
            v.wait_ge(s["y_mm"], 1)
            v.tensor_tensor(e.xt, e.bank(4), e.xt, ALU.add).then_inc(s["x_done"], 1)

        @block.gpsimd
        def _(g):
            for n in range(N):
                g.wait_ge(s["b_cp"], n + 1)
                for c in range(2):
                    if n >= 2:
                        g.wait_ge(s["hs_done"], 2 * (n - 2) + c + 1)
                    if n == 0:
                        g.wait_ge(s["du_done"], c + 1)
                    g.tensor_tensor(bu(c, n), du(c), bs(n), ALU.mult).then_inc(s["bu_done"], 1)


def dual_attention(nc, e, W):
    scale = float(D) ** -0.5
    names = LN_SEMS + ("pr_mm pr_cp v_mm v_cp s_mm s_sub ex_done p_done pt_mm pt_cp o_mm o_cp g_mm g_done z_done "
                       "zt_mm dve_own x_done")
    with block_of(nc, "dual_attention", names) as (block, s):
        ln = LayerNorm(e, s, e.xt, e.xn, e.eps5, dstT=e.xnT, bank=e.bank(7))
        pr = lambda i: e.w0[:, i * GT:(i + 1) * GT]
        vv = lambda i: e.w1[0:S, i * 1024:(i + 1) * 1024]
        p, pt = e.w2[:, 0:GT], e.w3[0:S, 0:1024]
        o = lambda i: e.w5[:, i * GT:(i + 1) * GT]
        gate, z = e.w6[:, 0:GT], e.w6[:, GT:2 * GT]
        mx, sm = e.sm[:, 0:8], e.sm[:, 8:16]

        @block.tensor
        def _(pe):
            ln.tensor(pe)
            pe.wait_ge(s["ln_xT"], 1)
            for i, (w, src) in enumerate((("Wq_c", e.xnT), ("Wk_s", e.ctxT), ("Wq_s", e.ctxT), ("Wk_c", e.xnT))):
                pe.matmul(e.bank(i), W(w), src, start=True, stop=True).then_inc(s["pr_mm"], 1)
            for i, (w, b_, src) in enumerate((("Wv_s", "bv_s", e.ctxT), ("Wv_c", "bv_c", e.xnT))):
                for b in range(NB):
                    out = e.bank(4 + 2 * i, 2)[0:S, b * D:(b + 1) * D]
                    pe.matmul(out, src[:, b * S:(b + 1) * S], W(w), start=True, stop=False)
                    ins = pe.matmul(out, e.ones[0:1, 0:S], W(b_), start=False, stop=True)
                ins.then_inc(s["v_mm"], 1)
            pe.wait_ge(s["pr_cp"], 4)
            for i in range(2):
                for b in range(NB):
                    col = slice(b * S, (b + 1) * S)
                    ins = pe.matmul(e.bank(0)[(b % 2) * S:(b % 2 + 1) * S, (i * NT + b // 2) * S:(i * NT + b // 2 + 1) * S],
                                    pr(2 * i)[:, col], pr(2 * i + 1)[:, col], start=True, stop=True)
            ins.then_inc(s["s_mm"], 1)
            pe.wait_ge(s["p_done"], 1)
            for k in range(2 * NT):
                ins = pe.transpose(e.bank(1, 2)[0:S, k * P:(k + 1) * P], p[:, k * S:(k + 1) * S], e.ident)
            ins.then_inc(s["pt_mm"], 1)
            pe.wait_ge(s["pt_cp"], 1)
            pe.wait_ge(s["v_cp"], 2)
            for i in range(2):
                for b in range(NB):
                    k = (i * NT + b // 2) * P + (b % 2) * S
                    ins = pe.matmul(e.bank(3 + i)[:, b * S:(b + 1) * S], vv(i)[:, b * D:(b + 1) * D], pt[:, k:k + S],
                                    start=True, stop=True)
                ins.then_inc(s["o_mm"], 1)
            pe.wait_ge(s["o_cp"], 2)
            for i in range(2):
                ins = pe.matmul(e.bank(5), W("Wg")[:, i * D:(i + 1) * D], o(i), start=(i == 0), stop=(i == 1))
            ins.then_inc(s["g_mm"], 1)
            pe.wait_ge(s["z_done"], 1)
            transpose_group(pe, e, e.bank(6), z).then_inc(s["zt_mm"], 1)

        @block.scalar
        def _(a):
            ln.scalar(a)
            for i in range(4):
                a.wait_ge(s["pr_mm"], i + 1)
                a.activation(pr(i), e.bank(i), ACT.Identity, bias=W("bqk")[:, i:i + 1]).then_inc(s["pr_cp"], 1)
            for i in range(2):
                a.wait_ge(s["v_mm"], i + 1)
                a.activation(vv(i), e.bank(4 + 2 * i, 2)[0:S, :], ACT.Copy).then_inc(s["v_cp"], 1)
            a.wait_ge(s["s_sub"], 1)
            a.activation(p, p, ACT.Exp, scale=scale).then_inc(s["ex_done"], 1)
            a.wait_ge(s["pt_mm"], 1)
            a.activation(pt, e.bank(1, 2)[0:S, :], ACT.Copy).then_inc(s["pt_cp"], 1)
            for i in range(2):
                a.wait_ge(s["o_mm"], i + 1)
                a.activation(o(i), e.bank(3 + i), ACT.Copy).then_inc(s["o_cp"], 1)
            a.wait_ge(s["g_mm"], 1)
            a.activation(gate, e.bank(5), ACT.Sigmoid, bias=W("bg")).then_inc(s["g_done"], 1)

        @block.vector
        def _(v):
            own = Chain(v, s["dve_own"])
            ln.vector(v)
            v.wait_ge(s["s_mm"], 1)
            own.step(v.tensor_reduce(mx, tiles(e.bank(0), 8), AX.X, ALU.max))
            v.tensor_tensor(tiles(p, 8), tiles(e.bank(0), 8), spread(mx, S), ALU.subtract).then_inc(s["s_sub"], 1)
            v.wait_ge(s["ex_done"], 1)
            own.step(v.tensor_reduce(sm, tiles(p, 8), AX.X, ALU.add))
            own.step(v.reciprocal(sm, sm))
            v.tensor_tensor(tiles(p, 8), tiles(p, 8), spread(sm, S), ALU.mult).then_inc(s["p_done"], 1)
            v.wait_ge(s["o_cp"], 2)
            own.step(v.tensor_tensor(z, o(0), o(1), ALU.subtract))
            v.wait_ge(s["g_done"], 1)
            own.step(v.tensor_tensor(z, z, gate, ALU.mult))
            v.tensor_tensor(z, z, o(1), ALU.add).then_inc(s["z_done"], 1)
            v.wait_ge(s["zt_mm"], 1)
            v.tensor_tensor(e.xt, e.bank(6), e.xt, ALU.add).then_inc(s["x_done"], 1)


QB, QEPS = 128.0, 1e-5


def quantised_max(nc, e, W):
    with block_of(nc, "quantised_max", LN_SEMS + LN2_SEMS + "dve_own") as (block, s):
        ln = LayerNorm(e, s, e.xt, e.xn, e.eps5)
        ln2 = LayerNorm(e, s, e.xn, e.w6[:, 0:GT], e.eps3, dstT=e.xnT, bank=e.bank(7), gain=W("ln_gamma"),
                        shift=W("ln_beta"), pre="ln2")

        @block.tensor
        def _(pe):
            ln2.tensor(pe)

        @block.scalar
        def _(a):
            ln.scalar(a)
            ln2.scalar(a)

        @block.vector
        def _(v):
            own = Chain(v, s["dve_own"])
            ln.vector(v)
            v.wait_ge(s["ln_xn"], NT)
            ln2.vector(v)
            v.wait_ge(s["ln2_xT"], 1)
            own.step(v.tensor_reduce(e.sm[:, 0:1], e.xnT, AX.X, ALU.max, apply_absolute_value=True))
            own.step(v.tensor_tensor(e.gmax, e.gmax, e.sm[:, 0:1], ALU.max))


def quantised_setup(nc, e, W):
    with block_of(nc, "quantised_setup", "late_loaded t_mm r_done b_mm abs_done bs_mm dve_own") as (block, s):
        row, tot = e.sm[0:1, 0:1], e.sm[:, 1:2]

        @block.sync
        def _(sp):
            for sb, dram in e.late_blobs:
                sp.dma_start(sb, dram).then_inc(s["late_loaded"], 16)
            sp.wait_ge(s["late_loaded"], 16 * len(e.late_blobs))

        @block.tensor
        def _(pe):
            pe.transpose(e.bank(0)[0:1, 0:P], e.gmax, e.ident).then_inc(s["t_mm"], 1)
            pe.wait_ge(s["r_done"], 1)
            pe.matmul(e.bank(1)[:, 0:1], e.ones[0:1, 0:P], row, start=True, stop=True).then_inc(s["b_mm"], 1)
            pe.wait_ge(s["abs_done"], 1)
            pe.matmul(e.bank(2)[:, 0:1], e.ones, tot, start=True, stop=True).then_inc(s["bs_mm"], 1)

        @block.vector
        def _(v):
            own = Chain(v, s["dve_own"])
            v.tensor_reduce(tot, W("weight"), AX.X, ALU.add, apply_absolute_value=True).then_inc(s["abs_done"], 1)
            v.wait_ge(s["t_mm"], 1)
            v.tensor_reduce(row, e.bank(0)[0:1, 0:P], AX.X, ALU.max).then_inc(s["r_done"], 1)
            v.wait_ge(s["b_mm"], 1)
            own.step(v.tensor_copy(e.qs[:, 0:1], e.bank(1)[:, 0:1]))
            own.step(v.reciprocal(e.qs[:, 1:2], e.qs[:, 0:1]))
            own.step(v.tensor_scalar(e.qs[:, 1:2], e.qs[:, 1:2], QB, None, ALU.mult))
            v.wait_ge(s["bs_mm"], 1)
            own.step(v.tensor_scalar(e.qs[:, 2:3], e.bank(2)[:, 0:1], 1.0 / (D * D), None, ALU.mult))
            own.step(v.tensor_scalar(e.qs[:, 3:4], e.qs[:, 2:3], QEPS, None, ALU.add))
            own.step(v.reciprocal(e.qs[:, 3:4], e.qs[:, 3:4]))
            own.step(v.tensor_scalar(e.wq, W("weight"), e.qs[:, 3:4], 1.0, ALU.mult, ALU.min))
            own.step(v.tensor_scalar(e.wq, e.wq, -1.0, 12582912.0, ALU.max, ALU.add))
            own.step(v.tensor_scalar(e.wq, e.wq, -12582912.0, None, ALU.add))
            own.step(v.tensor_scalar(e.qs[:, 4:5], e.qs[:, 0:1], e.qs[:, 2:3], 1.0 / QB, ALU.mult, ALU.mult))


def quantised_ffn(nc, e, W):
    with block_of(nc, "quantised_ffn", LN_SEMS + LN2_SEMS + "dve_own xq_done y_mm x_done") as (block, s):
        ln = LayerNorm(e, s, e.xt, e.xn, e.eps5)
        ln2 = LayerNorm(e, s, e.xn, e.w6[:, 0:GT], e.eps3, dstT=e.xnT, bank=e.bank(7), gain=W("ln_gamma"),
                        shift=W("ln_beta"), pre="ln2")

        @block.tensor
        def _(pe):
            ln2.tensor(pe)
            pe.wait_ge(s["xq_done"], 1)
            project_out(pe, e, e.bank(0), [(e.xnT, e.wq)], None).then_inc(s["y_mm"], 1)

        @block.scalar
        def _(a):
            ln.scalar(a)
            ln2.scalar(a)

        @block.vector
        def _(v):
            own = Chain(v, s["dve_own"])
            ln.vector(v)
            v.wait_ge(s["ln_xn"], NT)
            ln2.vector(v)
            v.wait_ge(s["ln2_xT"], 1)
            own.step(v.tensor_scalar(e.xnT, e.xnT, e.qs[:, 1:2], QB - QEPS, ALU.mult, ALU.min))
            v.tensor_scalar(e.xnT, e.xnT, -QB + QEPS, None, ALU.max).then_inc(s["xq_done"], 1)
            v.wait_ge(s["y_mm"], 1)
            v.scalar_tensor_tensor(out=e.xt, in0=e.bank(0), scalar=e.qs[:, 4:5], in1=e.xt, op0=ALU.mult,
                                   op1=ALU.add).then_inc(s["x_done"], 1)


def rwkv_attention(nc, e, W):
    names = LN_SEMS + ("xx_done mix_done rk_mm rk_cp rbd_done vg_mm v_cp g_done s_mm at_done o_mm sq_done std_done yn_done t_mm "
                       "t_cp y_mm dve_own x_done")
    with block_of(nc, "rwkv_attention", names) as (block, s):
        xp = tiles(e.xsh[:, 0:NB * (S + 1)], NB)
        ln = LayerNorm(e, s, e.xt, e.xn, e.eps5, dstT=xp[:, :, 1:S + 1], bank=e.bank(7))
        mix = lambda i: e.w5[:, i * GT:(i + 1) * GT] if i < 2 else e.w6[:, (i - 2) * GT:(i - 1) * GT]
        xx = e.w0[:, 0:GT]
        rk = lambda i: e.w0[:, (2 + i) * GT:(3 + i) * GT]
        rbd = lambda j: (e.w3, e.w4)[j % 2]
        vs, gs = e.w2[:, 0:GT], e.w2[:, GT:2 * GT]
        sbank = lambda j: e.bank(2 + 2 * (j % 2), 2)
        at = lambda j: e.w1[:, (j % 2) * 1024:(j % 2) * 1024 + 1024]
        y, sq, yT = e.w0[:, 0:GT], e.w0[:, GT:2 * GT], e.w5[:, 0:GT]
        mean, var = e.sm[:, 0:64], e.sm[:, 64:128]

        @block.tensor
        def _(pe):
            ln.tensor(pe)
            for i, w in enumerate(("Wr", "Wk")):
                pe.wait_ge(s["mix_done"], i + 1)
                pe.matmul(e.bank(i), W(w), mix(i), start=True, stop=True).then_inc(s["rk_mm"], 1)
            for i, w in enumerate(("Wv", "Wg")):
                pe.wait_ge(s["mix_done"], 3 + i)
                pe.wait_ge(s["rk_cp"], 1 + i)
                project_out(pe, e, e.bank(i), [(mix(2 + i), W(w))], None).then_inc(s["vg_mm"], 1)

            def scores(j):
                pe.wait_ge(s["rbd_done"], j + 1)
                if j >= 2:
                    pe.wait_ge(s["at_done"], j - 1)
                for b2 in range(2):
                    t = (2 * j + b2) * S
                    for i in range(2):
                        rhs = tiles(rbd(j), H)[:, i * 8:(i + 1) * 8, b2 * S:(b2 + 1) * S]
                        out = tiles(sbank(j)[b2 * S:(b2 + 1) * S, i * 512:(i + 1) * 512], 8)
                        ins = pe.matmul(out, rk(1)[:, t:t + S], rhs, start=True, stop=True)
                ins.then_inc(s["s_mm"], 1)

            pe.wait_ge(s["rk_cp"], 2)
            pe.wait_ge(s["v_cp"], 1)
            scores(0)
            scores(1)
            for j in range(NT):
                pe.wait_ge(s["at_done"], j + 1)
                for b2 in range(2):
                    r0 = slice(b2 * S, (b2 + 1) * S)
                    for h in range(H):
                        col = slice(j * D + h * HD, j * D + (h + 1) * HD)
                        ins = pe.matmul(e.bank(6)[r0, col], at(j)[r0, h * S:(h + 1) * S], vs[r0, col],
                                        start=True, stop=True)
                ins.then_inc(s["o_mm"], 1)
                if j + 2 < NT:
                    scores(j + 2)
            pe.wait_ge(s["yn_done"], 1)
            transpose_group(pe, e, e.bank(0), y).then_inc(s["t_mm"], 1)
            pe.wait_ge(s["t_cp"], 1)
            project_out(pe, e, e.bank(1), [(yT, W("Wo"))], None).then_inc(s["y_mm"], 1)

        @block.gpsimd
        def _(g):
            g.wait_ge(s["rk_cp"], 1)
            for j in range(NT):
                if j >= 2:
                    g.wait_ge(s["s_mm"], j - 1)
                g.tensor_tensor(tiles(rbd(j), H), repeat(rk(0)[:, j * P:(j + 1) * P], H), spread(e.hmask, P),
                                ALU.mult).then_inc(s["rbd_done"], 1)

        @block.scalar
        def _(a):
            ln.scalar(a)
            for i in range(2):
                a.wait_ge(s["rk_mm"], i + 1)
                a.activation(rk(i), e.bank(i), ACT.Copy).then_inc(s["rk_cp"], 1)
            a.wait_ge(s["vg_mm"], 1)
            a.activation(vs, e.bank(0), ACT.Copy).then_inc(s["v_cp"], 1)
            a.wait_ge(s["vg_mm"], 2)
            a.activation(gs, e.bank(1), ACT.Gelu).then_inc(s["g_done"], 1)
            a.wait_ge(s["sq_done"], 1)
            a.activation(var, var, ACT.Sqrt, bias=e.eps64).then_inc(s["std_done"], 1)
            a.wait_ge(s["t_mm"], 1)
            a.activation(yT, e.bank(0), ACT.Copy).then_inc(s["t_cp"], 1)

        @block.vector
        def _(v):
            own = Chain(v, s["dve_own"])
            ln.vector(v)
            v.wait_ge(s["ln_xT"], 1)
            own.step(v.tensor_tensor(tiles(xx, NB), xp[:, :, 0:S], xp[:, :, 1:S + 1], ALU.subtract))
            for i in range(4):
                v.scalar_tensor_tensor(out=tiles(mix(i), NB), in0=tiles(xx, NB), scalar=W("maa")[:, i:i + 1],
                                       in1=xp[:, :, 1:S + 1], op0=ALU.mult, op1=ALU.add).then_inc(s["mix_done"], 1)
            for j in range(NT):
                v.wait_ge(s["s_mm"], j + 1)
                if j >= 2:
                    v.wait_ge(s["o_mm"], j - 1)
                v.tensor_tensor(at(j), sbank(j), e.wmat, ALU.mult).then_inc(s["at_done"], 1)
            v.wait_ge(s["o_mm"], NT)
            g8 = lambda t: tiles(t, NT * H)
            own.step(v.tensor_reduce(mean, g8(e.bank(6)), AX.X, ALU.add))
            own.step(v.tensor_scalar(mean, mean, 1.0 / HD, None, ALU.mult))
            own.step(v.tensor_tensor(g8(y), g8(e.bank(6)), spread(mean, HD), ALU.subtract))
            own.step(v.tensor_tensor(sq, y, y, ALU.mult))
            own.step(v.tensor_reduce(var, g8(sq), AX.X, ALU.add))
            v.tensor_scalar(var, var, 1.0 / HD, None, ALU.mult).then_inc(s["sq_done"], 1)
            v.wait_ge(s["std_done"], 1)
            own.step(v.reciprocal(var, var))
            own.step(v.tensor_tensor(g8(y), g8(y), spread(var, HD), ALU.mult))
            own.step(v.tensor_tensor(tiles(y), tiles(y), repeat(W("ln_w"), NT), ALU.mult))
            own.step(v.tensor_tensor(tiles(y), tiles(y), repeat(W("ln_b"), NT), ALU.add))
            v.wait_ge(s["g_done"], 1)
            v.tensor_tensor(y, y, gs, ALU.mult).then_inc(s["yn_done"], 1)
            v.wait_ge(s["y_mm"], 1)
            v.tensor_tensor(e.xt, e.bank(1), e.xt, ALU.add).then_inc(s["x_done"], 1)


def top2_ffn(nc, e, W):
    names = LN_SEMS + LN2_SEMS + ("lg_mm lg_done ex_done w_done gt_mm gt_cp bb_mm dve_own up_mm act_done down_mm "
                                  "acc_done x_done")
    with block_of(nc, "top2_ffn", names) as (block, s):
        ln = LayerNorm(e, s, e.xt, e.xn, e.eps5, dstT=e.xnT, bank=e.bank(7))
        ln2 = LayerNorm(e, s, e.x2, e.xn, e.eps5, pre="ln2")
        lg, mx, keep, sm = e.sm[:, 0:32], e.sm[:, 32:36], e.sm[:, 40:72], e.sm[:, 36:40]
        gT = e.w5[0:E, 0:GT]

        @block.tensor
        def _(pe):
            ln.tensor(pe)
            pe.wait_ge(s["ln_xT"], 1)
            for j in range(NT):
                out = e.bank(6)[:, j * E:(j + 1) * E]
                pe.matmul(out, e.xnT[:, j * P:(j + 1) * P], W("gate_w"), start=True, stop=False)
                ins = pe.matmul(out, e.ones[0:1, 0:P], W("gate_b"), start=False, stop=True)
            ins.then_inc(s["lg_mm"], 1)

            def turn_weights():
                pe.wait_ge(s["w_done"], 1)
                for j in range(NT):
                    ins = pe.transpose(e.bank(7)[0:E, j * P:(j + 1) * P], lg[:, j * E:(j + 1) * E], e.ident)
                ins.then_inc(s["gt_mm"], 1)

            def output_biases():
                pe.wait_ge(s["gt_cp"], 1)
                for j in range(NT):
                    ins = pe.matmul(e.bank(6)[:, j * D:(j + 1) * D], gT[:, j * P:(j + 1) * P], W("b2"), start=True, stop=True)
                ins.then_inc(s["bb_mm"], 1)

            gelu_experts_tensor(pe, e, s, e.xnT, lambda x, f: W("w1")[:, (x * FC + f) * P:(x * FC + f + 1) * P],
                                lambda x, f: W("w2")[:, (x * FC + f) * D:(x * FC + f + 1) * D],
                                {}, {0: turn_weights, 1: output_biases})

        @block.scalar
        def _(a):
            ln.scalar(a)

            def numerators():
                a.wait_ge(s["lg_done"], 1)
                a.activation(lg, lg, ACT.Exp).then_inc(s["ex_done"], 1)

            def copy_weights():
                a.wait_ge(s["gt_mm"], 1)
                a.activation(gT, e.bank(7)[0:E, :], ACT.Copy).then_inc(s["gt_cp"], 1)

            gelu_experts_scalar(a, e, s, ACT.Gelu, lambda x, f: W("b1")[:, x * FC + f:x * FC + f + 1],
                                {0: numerators, 1: copy_weights})
            ln2.scalar(a)

        @block.vector
        def _(v):
            own = Chain(v, s["dve_own"])
            ln.vector(v)
            v.wait_ge(s["lg_mm"], 1)
            own.step(v.tensor_scalar(lg, e.bank(6)[:, 0:32], 1.0 / 0.9, None, ALU.mult))
            top_mask(v, own, e, lg, keep, NT, 2)
            own.step(v.tensor_reduce(mx, tiles(lg), AX.X, ALU.max))
            v.tensor_tensor(tiles(lg), tiles(lg), spread(mx, E), ALU.subtract).then_inc(s["lg_done"], 1)
            v.wait_ge(s["ex_done"], 1)
            own.step(v.tensor_tensor(lg, lg, keep, ALU.mult))
            own.step(v.tensor_reduce(sm, tiles(lg), AX.X, ALU.add))
            own.step(v.reciprocal(sm, sm))
            v.tensor_tensor(tiles(lg), tiles(lg), spread(sm, E), ALU.mult).then_inc(s["w_done"], 1)
            v.wait_ge(s["bb_mm"], 1)
            own.step(v.tensor_copy(e.x2, e.bank(6)))
            v.wait_ge(s["w_done"], 1)
            weighted_sum_vector(v, e, s, e.x2, lg, E, list(range(E)))
            ln2.vector(v)
            v.wait_ge(s["ln2_xn"], NT)
            own.step(v.tensor_tensor(tiles(e.xn), tiles(e.xn), repeat(W("ln_g"), NT), ALU.mult))
            own.step(v.tensor_tensor(tiles(e.xn), tiles(e.xn), repeat(W("ln_b"), NT), ALU.add))
            v.tensor_tensor(e.xt, e.xn, e.xt, ALU.add).then_inc(s["x_done"], 1)


def setup(nc, e, A):
    with block_of(nc, "setup", "loaded zeroed dve_own act_own l_done d_exp d_done w_exp w_done") as (block, s):
        n = len(e.blobs)
        L1, L2, L3 = e.W["L1_attn"], e.W["L2_attn"], e.W["L3_attn"]

        @block.sync
        def _(sp):
            for sb, dram in e.blobs:
                sp.dma_start(sb, dram).then_inc(s["loaded"], 16)
            sp.wait_ge(s["loaded"], 16 * n)

        @block.scalar
        def _(a):
            own = Chain(a, s["act_own"])
            a.wait_ge(s["loaded"], 16 * n)
            own.step(a.activation(e.nla, L1("alpha"), ACT.Exp, scale=-1.0))
            own.step(a.activation(e.nla, e.nla, ACT.Ln, bias=1.0))
            for c in range(WC):
                a.activation(e.pq[:, c * S:(c + 1) * S], e.xq, ACT.Exp, scale=e.nla[:, c:c + 1])
                a.activation(e.pk1[:, c * 32:(c + 1) * 32], e.xk[:, 32:S], ACT.Exp, scale=e.nla[:, c:c + 1])
                a.activation(e.pk2[:, c * S:(c + 1) * S], e.xk, ACT.Exp, scale=e.nla[:, c:c + 1])
            a.activation(e.aneg, L2("A_log"), ACT.Exp).then_inc(s["l_done"], 1)
            a.activation(e.dec, L3("decay"), ACT.Exp).then_inc(s["d_exp"], 1)
            a.wait_ge(s["d_done"], 1)
            for h in range(H):
                ins = a.activation(e.wmat[:, h * S:(h + 1) * S], e.expo, ACT.Exp, scale=e.dec[:, h:h + 1])
            ins.then_inc(s["w_exp"], 1)

        @block.vector
        def _(v):
            own = Chain(v, s["dve_own"])
            for t in (e.atz, e.xpad, e.xsh, e.adec, e.gmax):
                ins = v.memset(t, 0.0)
            ins.then_inc(s["zeroed"], 1)
            v.wait_ge(s["zeroed"], 1)
            v.wait_ge(s["loaded"], 16 * n)
            v.tensor_copy(e.half[:, 0:S], e.ident[:, 0:S])
            for i in range(3):
                v.tensor_copy(e.sel[i * 32:(i + 1) * 32, :], e.ident[0:32, 0:32])
            v.tensor_copy(e.half[:, S:2 * S], e.causal)
            v.wait_ge(s["l_done"], 1)
            own.step(v.tensor_scalar(e.aneg, e.aneg, -1.0, None, ALU.mult))
            v.wait_ge(s["d_exp"], 1)
            v.tensor_scalar(e.dec, e.dec, 1e30, -1.0, ALU.min, ALU.mult).then_inc(s["d_done"], 1)
            v.wait_ge(s["w_exp"], 1)
            own.step(v.tensor_tensor(tiles(e.wmat, H), tiles(e.wmat, H), repeat(e.strict, H), ALU.mult))
            for h in range(H):
                w = e.wmat[:, h * S:(h + 1) * S]
                ins = v.scalar_tensor_tensor(out=w, in0=e.eye, scalar=L3("faaaa")[:, h:h + 1], in1=w, op0=ALU.mult,
                                             op1=ALU.add)
            own.step(ins)


def load_group(nc, title, e, g, src, ctx, mask):
    with block_of(nc, title, "x_in c_in m_in t_mm t_cp k_done") as (block, s):
        rows = lambda t: t[bass.ts(g, GT), :].rearrange("(j p) d -> p j d", p=P)

        @block.sync
        def _(sp):
            sp.dma_start(tiles(e.w5[:, 0:GT]), rows(ctx)).then_inc(s["c_in"], 16)
            sp.dma_start(tiles(e.xt), rows(src)).then_inc(s["x_in"], 16)
            if mask is not None:
                for b2 in range(2):
                    m = mask[bass.ts(g, NB), :].rearrange("(j b) k -> b j k", b=2)[b2].partition_broadcast(S)
                    sp.dma_start(tiles(e.kmask[b2 * S:(b2 + 1) * S, :]), m).then_inc(s["m_in"], 16)
            sp.wait_ge(s["x_in"], 16)

        @block.tensor
        def _(pe):
            pe.wait_ge(s["c_in"], 16)
            transpose_group(pe, e, e.bank(0), e.w5[:, 0:GT]).then_inc(s["t_mm"], 1)

        @block.scalar
        def _(a):
            a.wait_ge(s["t_mm"], 1)
            a.activation(e.ctxT, e.bank(0), ACT.Copy).then_inc(s["t_cp"], 1)

        @block.vector
        def _(v):
            if mask is not None:
                v.wait_ge(s["m_in"], 32)
                v.tensor_scalar(e.kmask, e.kmask, -1.0, 10000.0 * float(HD) ** 0.5, ALU.add, ALU.mult).then_inc(s["k_done"], 1)


def norm_context(nc, e, W):
    with block_of(nc, "norm_context", LN_SEMS) as (block, s):
        ln = LayerNorm(e, s, e.w5[:, 0:GT], e.xn, e.eps5, dstT=e.ctxT, bank=e.bank(7), gain=W("ln1_g"), shift=W("ln1_b"))

        @block.tensor
        def _(pe):
            ln.tensor(pe)

        @block.scalar
        def _(a):
            ln.scalar(a)

        @block.vector
        def _(v):
            ln.vector(v)


def store_group(nc, title, e, g, out):
    with block_of(nc, title, "x_out") as (block, s):
        @block.sync
        def _(sp):
            sp.dma_start(out[bass.ts(g, GT), :].rearrange("(j p) d -> p j d", p=P), tiles(e.xt)).then_inc(s["x_out"], 16)
            sp.wait_ge(s["x_out"], 16)


def decoder(nc, drams, packs, x, ctx_rows, mask, out):
    groups = x.shape[0] // GT
    with ExitStack() as stack:
        def sb(name, n):
            return stack.enter_context(nc.sbuf_tensor(name, [P, n], F32))

        ps = stack.enter_context(nc.psum_tensor("ps", [P, 8 * 512], F32))
        blobs, late_blobs, W, held = [], [], {}, {}
        for name, dram in drams.items():
            n = dram.shape[1]
            if name in LATE:
                t = held[LATE[name]]
                late_blobs.append((t[:, 0:n], dram))
            else:
                later = [drams[k].shape[1] for k, first in LATE.items() if first == name]
                t = held[name] = sb(name + "_w", max([n] + later))
                blobs.append((t[:, 0:n], dram))
            places = packs[name]
            W[name] = lambda key, t=t, places=places: t[0:places[key][0], places[key][1]:places[key][1] + places[key][2]]
        e = Buffers()
        e.bank = lambda b, n=1: ps[:, b * 512:(b + n) * 512]
        e.blobs, e.late_blobs, e.W = blobs, late_blobs, W
        e.ident = W["const"]("ident")
        e.ones = W["const"]("ones")
        e.cos = W["const"]("cos")
        e.sin = W["const"]("sin")
        e.hmask = W["const"]("hmask")
        e.causal = W["const"]("causal")
        e.vmask = W["const"]("vmask")
        e.headcol = W["const"]("headcol")
        e.tri = W["const"]("tri")
        e.strict = W["const"]("strict")
        e.eye = W["const"]("eye")
        e.expo = W["const"]("expo")
        e.headblk = W["const"]("headblk")
        e.bsel = W["const"]("bsel")
        e.lower = W["const"]("lower")
        e.xq = W["const"]("xq")
        e.xk = W["const"]("xk")
        e.eps5 = W["const"]("eps5")
        e.eps3 = W["const"]("eps3")
        e.eps64 = W["const"]("eps64")
        e.half = stack.enter_context(nc.sbuf_tensor("half", [P, 2 * S], BF16))[:, :]
        e.sel = stack.enter_context(nc.sbuf_tensor("sel", [96, 32], BF16))[:, :]
        e.bcp = stack.enter_context(nc.sbuf_tensor("bcp", [96, GT], BF16))[:, :]
        e.bcm = stack.enter_context(nc.sbuf_tensor("bcm", [32, GT], BF16))[:, :]
        e.xt = sb("xt", GT)[:, :]
        e.xn = sb("xn", GT)[:, :]
        e.x2 = sb("x2", GT)[:, :]
        e.xnT = sb("xnT", GT)[:, :]
        e.ctxT = sb("ctxT", GT)[:, :]
        e.st = sb("st", 6 * NT)[:, :]
        e.mv = sb("mv", 2 * NT)[:, :]
        e.sd = sb("sd", NT)[:, :]
        e.rs = sb("rs", NT)[:, :]
        e.sm = sb("sm", 128)[:, :]
        e.kmask = sb("kmask", NT * S)[:, :]
        e.gmax = sb("gmax", 1)[:, :]
        e.qs = sb("qs", 8)[:, :]
        e.wq = sb("wq", D)[:, :]
        e.nla = sb("nla", WC)[:, :]
        e.pq = sb("pq", WC * S)[:, :]
        e.pk1 = sb("pk1", WC * 32)[:, :]
        e.pk2 = sb("pk2", WC * S)[:, :]
        e.aneg = sb("aneg", 32)[:, :]
        e.dec = sb("dec", H)[:, :]
        e.wmat = sb("wmat", H * S)[:, :]
        e.atz = sb("atz", 2 * GT)[:, :]
        e.xpad = sb("xpad", 2 * NB * (S + 3))[:, :]
        e.xsh = sb("xsh", NB * (S + 1))[:, :]
        e.adec = sb("adec", 4 * GT)[:, :]
        e.w0 = sb("w0", 2048)[:, :]
        e.w1 = sb("w1", 2048)[:, :]
        e.w2 = sb("w2", 2048)[:, :]
        e.w3 = sb("w3", 2048)[:, :]
        e.w4 = sb("w4", 2048)[:, :]
        e.w5 = sb("w5", 1024)[:, :]
        e.w6 = sb("w6", 1024)[:, :]
        setup(nc, e, None)
        with nc.Fori(0, groups) as g:
            load_group(nc, "load_a", e, g, x, ctx_rows, mask)
            if 1 in STAGES:
                w = W["L0_attn"]
                softmax_attention(nc, "self0", e, e.x2, e.w6[:, 0:GT], e.xnT, w("v"), None, w("proj"), w("b_proj"),
                                  causal=True, project=[(w("q"), e.xnT), (w("k"), e.xnT)])
            if 2 in STAGES:
                w = W["L0_xattn"]
                rope = {"mm": [(w("Wq"), e.xnT), (w("Wq_rot"), e.xnT), (w("Wk"), e.ctxT), (w("Wk_rot"), e.ctxT)],
                        "bias": [(w("bq"), w("bq_rot")), (w("bk"), w("bk_rot"))]}
                softmax_attention(nc, "cross0", e, e.xn, e.x2, e.ctxT, w("Wv"), w("bv"), w("Wo"), w("bo"),
                                  rope=rope)
            if 3 in STAGES:
                zone_ffn(nc, e, W["L0_ffn"])
            if 4 in STAGES:
                decay_attention(nc, e, W["L1_attn"])
            if 5 in STAGES:
                softmax_attention(nc, "cross1", e, e.xnT, e.ctxT, e.ctxT, e.ident, None,
                                  W["L1_xattn"]("W_o"), None, key_mask=True)
            if 6 in STAGES:
                top1_ffn(nc, e, W["L1_ffn"])
            if 7 in STAGES:
                state_space(nc, e, W["L2_attn"])
            if 8 in STAGES:
                dual_attention(nc, e, W["L2_xattn"])
            if 9 in STAGES:
                quantised_max(nc, e, W["L2_ffn"])
            store_group(nc, "store_a", e, g, out)
        if max(STAGES) >= 9:
            quantised_setup(nc, e, W["L2_ffn"])
            with nc.Fori(0, groups) as g:
                load_group(nc, "load_b", e, g, out, ctx_rows, None)
                norm_context(nc, e, W["L3_xattn"])
                if 9 in STAGES:
                    quantised_ffn(nc, e, W["L2_ffn"])
                if 10 in STAGES:
                    rwkv_attention(nc, e, W["L3_attn"])
                if 11 in STAGES:
                    norm_attention_mlp(nc, e, W["L3_xattn"])
                if 12 in STAGES:
                    top2_ffn(nc, e, W["L3_ffn"])
                store_group(nc, "store_b", e, g, out)


def kernel(**inputs):
    import numpy as np
    import concourse.bacc as bacc
    from concourse.bass_utils import run_bass_kernel_spmd

    I = {k: np.asarray(v) for k, v in inputs.items()}

    def chunks(a):
        c = a.shape[0] // P
        return a.reshape(c, P, -1).transpose(1, 0, 2).reshape(P, -1)

    def cols(a):
        return a.reshape(-1, P).T

    def row(a):
        return a.reshape(1, -1)

    turn = np.arange(D).reshape(H, 2, HD // 2)[:, ::-1].reshape(D)
    everyone = lambda a: np.repeat(a.reshape(1, -1), P, axis=0)
    half = lambda a, h: a.reshape(P, 3, D)[:, h]
    packs_in = {
        "L0_attn": {"q": half(I["L0_attn_w_qkv"], 0), "k": half(I["L0_attn_w_qkv"], 1),
                    "v": half(I["L0_attn_w_qkv"], 2), "proj": I["L0_attn_w_proj"], "b_proj": row(I["L0_attn_b_proj"])},
        "L0_xattn": {"Wq": I["L0_xattn_Wq"].T, "Wq_rot": I["L0_xattn_Wq"][turn].T, "Wk": I["L0_xattn_Wk"].T,
                     "Wk_rot": I["L0_xattn_Wk"][turn].T, "Wv": I["L0_xattn_Wv"].T, "Wo": I["L0_xattn_Wo"].T,
                     "bq": cols(I["L0_xattn_bq"]), "bq_rot": cols(I["L0_xattn_bq"][turn]), "bk": cols(I["L0_xattn_bk"]),
                     "bk_rot": cols(I["L0_xattn_bk"][turn]), "bv": row(I["L0_xattn_bv"]), "bo": row(I["L0_xattn_bo"])},
        "L0_ffn": {"W1": I["L0_ffn_W1"], "b1": I["L0_ffn_b1"].reshape(-1, 1), "W2": I["L0_ffn_W2"],
                   "b2": row(I["L0_ffn_b2"]),
                   "Wa": I["L0_ffn_Wa"].transpose(1, 0, 2).reshape(P, -1),
                   "Wb": chunks(I["L0_ffn_Wb"].reshape(-1, D))},
        "L1_attn": {"WQ": I["L1_attn_WQ"].T, "WK": I["L1_attn_WK"].T, "WV": I["L1_attn_WV"].T, "Wg": I["L1_attn_Wg"].T,
                    "WO": chunks(I["L1_attn_WO"].T), "bQ": cols(I["L1_attn_bQ"]), "bK": cols(I["L1_attn_bK"]),
                    "bg": cols(I["L1_attn_bg"]), "bV": row(I["L1_attn_bV"]), "bO": row(I["L1_attn_bO"]),
                    "ln_gamma": cols(I["L1_attn_ln_gamma"]), "ln_beta": cols(I["L1_attn_ln_beta"]),
                    "alpha": cols(I["L1_attn_alpha_logit"].reshape(-1))},
        "L1_xattn": {"W_o": I["L1_xattn_W_o"]},
        "L1_ffn": {"gate_w": I["L1_ffn_gate_w"], "sh_gate": I["L1_ffn_sh_gate"], "sh_up": I["L1_ffn_sh_up"],
                   "sh_down": chunks(I["L1_ffn_sh_down"]),
                   "rt_gate": I["L1_ffn_rt_gate"].transpose(1, 0, 2).reshape(P, -1),
                   "rt_up": I["L1_ffn_rt_up"].transpose(1, 0, 2).reshape(P, -1),
                   "rt_down": chunks(I["L1_ffn_rt_down"].reshape(-1, D))},
        "L2_attn": {"w_in": I["L2_attn_w_in"], "b_in": cols(I["L2_attn_b_in"]), "w_conv": chunks(I["L2_attn_w_conv"].T),
                    "b_conv": cols(I["L2_attn_b_conv"]), "w_x": chunks(I["L2_attn_w_x"]), "w_dt": I["L2_attn_w_dt"],
                    "A_log": chunks(I["L2_attn_A_log"]), "D": cols(I["L2_attn_D"]), "w_out": chunks(I["L2_attn_w_out"])},
        "L2_xattn": {**{k: I["L2_xattn_" + k].T for k in ("Wq_c", "Wk_s", "Wv_s", "Wq_s", "Wk_c", "Wv_c")},
                     "Wg": chunks(I["L2_xattn_Wg"].T), "bg": cols(I["L2_xattn_bg"]),
                     "bqk": np.stack([I["L2_xattn_" + k] for k in ("bq_c", "bk_s", "bq_s", "bk_c")], axis=1),
                     "bv_s": row(I["L2_xattn_bv_s"]), "bv_c": row(I["L2_xattn_bv_c"])},
        "L2_ffn": {"weight": I["L2_ffn_weight"], "ln_gamma": cols(I["L2_ffn_ln_gamma"]),
                   "ln_beta": cols(I["L2_ffn_ln_beta"])},
        "L3_attn": {"Wr": I["L3_attn_Wr"].T, "Wk": I["L3_attn_Wk"].T, "Wv": I["L3_attn_Wv"].T,
                    "Wg": I["L3_attn_Wg"].T, "Wo": I["L3_attn_Wo"].T,
                    "maa": np.stack([I["L3_attn_time_maa_" + k].reshape(-1) for k in "rkvg"], axis=1),
                    "decay": everyone(I["L3_attn_time_decay"]), "faaaa": everyone(I["L3_attn_time_faaaa"]),
                    "ln_w": everyone(I["L3_attn_ln_w"]), "ln_b": everyone(I["L3_attn_ln_b"])},
        "L3_xattn": {"wq": I["L3_xattn_wq"], "wk": I["L3_xattn_wk"], "wv": I["L3_xattn_wv"], "wo": chunks(I["L3_xattn_wo"]),
                     "bo": row(I["L3_xattn_bo"]), "w1": I["L3_xattn_w1"], "b1": cols(I["L3_xattn_b1"]),
                     "w2": chunks(I["L3_xattn_w2"]), "b2": row(I["L3_xattn_b2"]),
                     "ln1_g": cols(I["L3_xattn_ln1_g"]), "ln1_b": cols(I["L3_xattn_ln1_b"]),
                     "ln2_g": cols(I["L3_xattn_ln2_g"]), "ln2_b": cols(I["L3_xattn_ln2_b"])},
        "L3_ffn": {"gate_w": I["L3_ffn_gate_w"], "gate_b": row(I["L3_ffn_gate_b"]),
                   "w1": I["L3_ffn_w1"].transpose(1, 0, 2).reshape(P, -1), "b1": cols(I["L3_ffn_b1"].reshape(-1)),
                   "w2": chunks(I["L3_ffn_w2"].reshape(-1, D)), "b2": I["L3_ffn_b2"],
                   "ln_g": everyone(I["L3_ffn_ln_g"]), "ln_b": everyone(I["L3_ffn_ln_b"])},
    }
    p, t64 = np.arange(P), np.arange(S)
    pm = p % S
    inv = 1.0 / 10000.0 ** (np.arange(0, HD, 2, dtype=np.float32) / np.float32(HD))
    ang = (t64[None, :].astype(np.float32) * np.tile(inv.astype(np.float32), P // (HD // 2))[:, None])
    sign = np.where(p % HD < HD // 2, -1.0, 1.0)[:, None]
    one = np.ones((P, 1), np.float32)
    tok = np.arange(GT)
    packs_in["const"] = {
        "ident": np.eye(P), "ones": np.ones((P, P)), "hmask": (p[:, None] // HD == np.arange(H)[None, :]) * 1.0,
        "cos": np.cos(ang), "sin": np.sin(ang) * sign,
        "causal": np.where(t64[None, :] <= pm[:, None], 0.0, -1e30),
        "vmask": (p[:, None] // S == np.arange(2 * HD)[None, :] // HD) * 1.0,
        "headcol": (p[:, None] // S == np.arange(2)[None, :]) * 1.0,
        "tri": (pm[:, None] <= t64[None, :]) * 1.0,
        "strict": (pm[:, None] < t64[None, :]) * 1.0, "eye": (pm[:, None] == t64[None, :]) * 1.0,
        "expo": np.maximum(t64[None, :] - pm[:, None] - 1, 0) * 1.0,
        "headblk": (p[:, None] // S == p[None, :] // S) * 1.0,
        "bsel": (np.arange(NB)[:, None] == tok[None, :] // S) * 1.0,
        "lower": everyone((np.arange(8)[None, :] < np.arange(8)[:, None]) * 1.0),
        "xq": everyone(-((t64 % 32) - 16.0)), "xk": everyone(-(48.0 - t64)),
        "eps5": one * 1e-5, "eps3": one * 1e-3, "eps64": one * 64e-5,
    }
    nc = bacc.Bacc("TRN2", target_bir_lowering=False, num_devices=1)
    arrays, drams, packs = {}, {}, {}
    for name, parts in packs_in.items():
        places, at = {}, 0
        for key, a in parts.items():
            places[key] = (a.shape[0], at, a.shape[1])
            at += a.shape[1]
        blob = np.zeros((P, at), np.float32)
        for key, a in parts.items():
            n, o, w = places[key]
            blob[0:n, o:o + w] = a
        arrays[name] = blob
        packs[name] = places
        drams[name] = nc.dram_tensor(name, blob.shape, F32, kind="ExternalInput").ap()
    B = I["x"].shape[0]
    more = {"x": I["x"].reshape(B * S, D), "ctx": I["ctx_1024"].reshape(B * S, D), "mask": I["mask_BxS2_ff1"]}
    aps = {}
    for name, a in more.items():
        arrays[name] = np.ascontiguousarray(a)
        aps[name] = nc.dram_tensor(name, a.shape, F32, kind="ExternalInput").ap()
    out = nc.dram_tensor("out", (B * S, D), F32, kind="ExternalOutput").ap()
    decoder(nc, drams, packs, aps["x"], aps["ctx"], aps["mask"], out)
    r = run_bass_kernel_spmd(nc, [arrays], core_ids=[0])
    return r.results[0]["out"].reshape(B, S, D)
```
